# Optimizing a Trainium2 kernel written in Bass

```python
import numpy as np
import jax
import jax.numpy as jnp

def _softmax(x, axis=-1):
    return jax.nn.softmax(x, axis=axis)

def _gelu(x):
    return jax.nn.gelu(x, approximate=True)

def _silu(x):
    return jax.nn.silu(x)

def _sigmoid(x):
    return jax.nn.sigmoid(x)

def _layernorm(x, axis=-1, eps=1e-05):
    m = jnp.mean(x, axis=axis, keepdims=True)
    v = jnp.var(x, axis=axis, keepdims=True)
    return (x - m) / jnp.sqrt(v + eps)

def _scatter_add(tgt, idx, src, axis=0):
    return tgt.at[idx].add(src)

def _segment_sum(src, seg, n):
    return jax.ops.segment_sum(src, seg, n)
kernel_name = 'mk_macaron_d1_jaxref_r4_55c593'

def setup_inputs(seed: int=0):
    np.random.seed(seed)
    _w = jnp.asarray

    def _L0_attn_setup():
        import jax, jax.numpy as jnp
        import numpy as np
        B, L, D = (4, 512, 512)
        E, N, DT, DC = (1024, 16, 128, 4)
        EPS = 1e-05
        key = jax.random.key(seed)
        ks = jax.random.split(key, 12)
        s = lambda k, shape, scale: jax.random.normal(k, shape, jnp.float32) * scale
        return {'x': jax.random.normal(ks[0], (B, L, D), jnp.float32), 'norm_w': jnp.ones((D,), jnp.float32), 'W_skip': s(ks[1], (E, D), 0.02), 'W_in': s(ks[2], (E, D), 0.02), 'conv_w': s(ks[3], (E, 1, DC), 0.1), 'conv_b': jnp.zeros((E,), jnp.float32), 'Wd1': s(ks[4], (DT, E), 0.02), 'Wd2': s(ks[5], (E, DT), 0.02), 'bd2': jnp.zeros((E,), jnp.float32), 'WB': s(ks[6], (N, E), 0.02), 'WC': s(ks[7], (N, E), 0.02), 'A_log': s(ks[8], (E, N), 0.5), 'W_D': jnp.ones((E,), jnp.float32), 'W_out': s(ks[9], (D, E), 0.02)}
    _L0_attn_in = _L0_attn_setup()

    def _L0_ffn_setup():
        import jax, jax.numpy as jnp
        import numpy as np

        def _sparsify_2to4(h):
            B, S, I = h.shape
            g = h.reshape(B, S, I // 4, 4)
            a = jnp.abs(g)
            _, idx = jax.lax.top_k(a, 2)
            pos = jnp.arange(4)
            mask = (pos == idx[..., 0:1]) | (pos == idx[..., 1:2])
            return (g * mask.astype(g.dtype)).reshape(B, S, I)
        key = jax.random.key(seed)
        k1, k2, k3, k4 = jax.random.split(key, 4)
        B, S, H, I = (4, 512, 512, 2048)
        x = jax.random.normal(k1, (B, S, H), dtype=jnp.float32)
        w_gate = jax.random.normal(k2, (H, I), dtype=jnp.float32) / np.sqrt(H)
        w_up = jax.random.normal(k3, (H, I), dtype=jnp.float32) / np.sqrt(H)
        w_down = jax.random.normal(k4, (I, H), dtype=jnp.float32) / np.sqrt(I)
        return {'x': x, 'w_gate': w_gate, 'w_up': w_up, 'w_down': w_down}
    _L0_ffn_in = _L0_ffn_setup()
    _d = {'L0_attn_x': _L0_attn_in['x'], 'L0_attn_norm_w': _L0_attn_in['norm_w'], 'L0_attn_W_skip': _L0_attn_in['W_skip'], 'L0_attn_W_in': _L0_attn_in['W_in'], 'L0_attn_conv_w': _L0_attn_in['conv_w'], 'L0_attn_conv_b': _L0_attn_in['conv_b'], 'L0_attn_Wd1': _L0_attn_in['Wd1'], 'L0_attn_Wd2': _L0_attn_in['Wd2'], 'L0_attn_bd2': _L0_attn_in['bd2'], 'L0_attn_WB': _L0_attn_in['WB'], 'L0_attn_WC': _L0_attn_in['WC'], 'L0_attn_A_log': _L0_attn_in['A_log'], 'L0_attn_W_D': _L0_attn_in['W_D'], 'L0_attn_W_out': _L0_attn_in['W_out'], 'L0_ffn_w_gate': _L0_ffn_in['w_gate'], 'L0_ffn_w_up': _L0_ffn_in['w_up'], 'L0_ffn_w_down': _L0_ffn_in['w_down']}
    _x0 = _d['L0_attn_x']
    _d['L0_attn_x'] = jax.random.normal(jax.random.fold_in(jax.random.key(seed), 1), (8, 512, 512), dtype=_x0.dtype)
    del _x0
    return _d

def reference(L0_attn_x, L0_attn_norm_w, L0_attn_W_skip, L0_attn_W_in, L0_attn_conv_w, L0_attn_conv_b, L0_attn_Wd1, L0_attn_Wd2, L0_attn_bd2, L0_attn_WB, L0_attn_WC, L0_attn_A_log, L0_attn_W_D, L0_attn_W_out, L0_ffn_w_gate, L0_ffn_w_up, L0_ffn_w_down):

    def _L0_attn_ref(x, norm_w, W_skip, W_in, conv_w, conv_b, Wd1, Wd2, bd2, WB, WC, A_log, W_D, W_out):
        import jax, jax.numpy as jnp
        import numpy as np
        B, L, D = (4, 512, 512)
        E, N, DT, DC = (1024, 16, 128, 4)
        EPS = 1e-05
        xn = x * jax.lax.rsqrt(jnp.mean(x * x, axis=-1, keepdims=True) + EPS) * norm_w
        skip = xn @ W_skip.T
        u = xn @ W_in.T
        uc = jax.lax.conv_general_dilated(u.transpose(0, 2, 1), conv_w, (1,), [(DC - 1, 0)], dimension_numbers=('NCH', 'OIH', 'NCH'), feature_group_count=E)
        u = jax.nn.silu(uc.transpose(0, 2, 1) + conv_b)
        delta = jax.nn.softplus(u @ Wd1.T @ Wd2.T + bd2)
        Bt = u @ WB.T
        Ct = u @ WC.T
        A = -jnp.exp(A_log)

        def step(h, inps):
            d_l, b_l, c_l, u_l = inps
            h = jnp.exp(d_l[..., None] * A) * h + (d_l * u_l)[..., None] * b_l[:, None, :]
            y_l = jnp.einsum('ben,bn->be', h, c_l)
            return (h, y_l)
        h0 = jnp.zeros((x.shape[0], E, N), u.dtype)
        _, ys = jax.lax.scan(step, h0, (delta.transpose(1, 0, 2), Bt.transpose(1, 0, 2), Ct.transpose(1, 0, 2), u.transpose(1, 0, 2)))
        y = ys.transpose(1, 0, 2)
        y = (y + u * W_D) * jax.nn.silu(skip)
        return y @ W_out.T

    def _L0_ffn_ref(x, w_gate, w_up, w_down):
        import jax, jax.numpy as jnp
        import numpy as np

        def _sparsify_2to4(h):
            B, S, I = h.shape
            g = h.reshape(B, S, I // 4, 4)
            a = jnp.abs(g)
            _, idx = jax.lax.top_k(a, 2)
            pos = jnp.arange(4)
            mask = (pos == idx[..., 0:1]) | (pos == idx[..., 1:2])
            return (g * mask.astype(g.dtype)).reshape(B, S, I)
        h = jax.nn.silu(jnp.einsum('bsh,hi->bsi', x, w_gate)) * jnp.einsum('bsh,hi->bsi', x, w_up)
        h_sparse = _sparsify_2to4(h)
        return jnp.einsum('bsi,ih->bsh', h_sparse, w_down)
    x = L0_attn_x
    x = x + 0.5 * _L0_ffn_ref(_layernorm(x, axis=-1), L0_ffn_w_gate, L0_ffn_w_up, L0_ffn_w_down)
    x = x + _L0_attn_ref(_layernorm(x, axis=-1), L0_attn_norm_w, L0_attn_W_skip, L0_attn_W_in, L0_attn_conv_w, L0_attn_conv_b, L0_attn_Wd1, L0_attn_Wd2, L0_attn_bd2, L0_attn_WB, L0_attn_WC, L0_attn_A_log, L0_attn_W_D, L0_attn_W_out)
    x = x + 0.5 * _L0_ffn_ref(_layernorm(x, axis=-1), L0_ffn_w_gate, L0_ffn_w_up, L0_ffn_w_down)
    return x

_drawn_inputs = setup_inputs


def setup_inputs(seed=0):
    import zlib

    import numpy as np

    out = dict(_drawn_inputs(seed))
    spreads = {'L0_attn_norm_w': (1.0, 0.2),
     'L0_attn_conv_b': (0.0, 0.1),
     'L0_attn_bd2': (0.0, 0.1),
     'L0_attn_W_D': (1.0, 0.2)}
    factors = {}
    for name, (base, spread) in spreads.items():
        noise = np.random.default_rng([zlib.crc32(name.encode()), seed]).standard_normal(out[name].shape)
        drawn = base * np.exp(spread * noise) if base else spread * noise
        out[name] = jnp.asarray(drawn.astype(out[name].dtype))
    for name, factor in factors.items():
        out[name] = (out[name] * factor).astype(out[name].dtype)
    return out
```

```python
import numpy as np
import concourse.bass as bass
from concourse import mybir
from contextlib import ExitStack

B, L, D = 8, 512, 512
E, N, DT, DC = 1024, 16, 128, 4
I = 2048
P = 128
KD = D // P
KE = E // P
QUADS = I // (4 * P)
UNITS = N * KE
PIECE = KD * L
EPS = 1e-05
C_NORM, C_CW, C_CB, C_BD, C_AL, C_WD = 0, KD, KD + KE * DC, KD + KE * DC + KE, KD + KE * DC + 2 * KE, KD + KE * DC + 2 * KE + KE * N
SMALL = C_WD + KE

BANK_SK = [e % 4 for e in range(KE)]
BANK_OUT = [t for t in range(KD)]
BANK_IN = [e % 4 for e in range(KE)]
BANK_DT, BANK_BC = 0, 1
BANK_DL = [(e + 2) % 4 for e in range(KE)]
PROJ_JOBS = 2 * KE + 2
OUTP_JOBS = KE + KD


class Walk:

    def __init__(self):
        self.n = {}
        self.reg = None
        self.start = None
        self.per = {}

    def count(self, name):
        return self.n.get(name, 0)

    def add(self, name, k=1):
        self.n[name] = self.count(name) + k

    def enter(self, reg, per):
        self.reg, self.per, self.start = reg, per, dict(self.n)

    def leave(self, reps):
        for name, v in self.n.items():
            d = v - self.start.get(name, 0)
            assert d == self.per.get(name, d), (name, d)
            self.n[name] = v + (reps - 1) * d
        self.reg = None

    def at(self, name, value=None):
        value = self.count(name) if value is None else value
        if self.reg is None or not self.per.get(name):
            return max(value, 0)
        return self.reg * self.per[name] + value


def per_body():
    per = {"product_ready": 8 * 4 * 2 + OUTP_JOBS + PROJ_JOBS, "down_ready": 2 * (2 + 4 * QUADS) + 2, "magnitude_ready": 8 * 4, "hidden_ready": 8}
    per["down_read"] = per["down_ready"]
    banks = BANK_SK + BANK_OUT + BANK_IN + [BANK_DT, BANK_BC] + BANK_DL
    for b in range(4):
        per[f"bank_read_{b}"] = 16 + banks.count(b)
    per["dve_step"] = 2 + 4 + 2 * QUADS * 3 + KE * (DC - 1) + 2
    per.update({"squares_ready": 3, "variance_ready": 2, "root_ready": 4, "normed_ready": 3, "act_step": 2})
    per.update({"decay_ready": UNITS, "input_ready": UNITS, "state_ready": UNITS, "weighted_ready": UNITS, "sum_ready": UNITS})
    per.update({"gated_ready": KE, "conv_ready": KE, "u_ready": KE, "log_ready": 2, "delta_ready": 2, "first_term_ready": 2})
    for c in "gud":
        for k in range(2):
            per[f"loaded_{c}{k}"] = 16 * 5
    per.update({"bc_loaded_0": 32 * N // 2, "bc_loaded_1": 32 * N // 2, "bc_stored": 16, "x_loaded": 16, "x1_loaded": 16, "out_stored": 16, "x1_stored": 16})
    return per


def dn_order(kinds):
    order = []
    for s, kind in enumerate(kinds):
        if kind and s % 4 == 0:
            order += [("norm", s, 0), ("norm", s, 1)]
        if s > 0 and kinds[s - 1]:
            order += [("down", s - 1, t) for t in range(KD)]
    if kinds[-1]:
        order += [("down", len(kinds) - 1, t) for t in range(KD)]
    return order


def build(nc, x_in, ffn_w, mam_w, wdt_in, wbc_in, wd2_in, small_in, out):
    f32, bf16 = mybir.dt.float32, mybir.dt.bfloat16
    ALU, ACT = mybir.AluOpType, mybir.ActivationFunctionType
    ctx = ExitStack()
    PER = per_body()
    FULL = ["F"] * 4 + ["G"] * 4

    with ctx:
        def sb(name, shape, dt=f32):
            return ctx.enter_context(nc.sbuf_tensor(name, shape, dt))

        def pb(name):
            return ctx.enter_context(nc.psum_tensor(name, [P, L], f32))

        bc_dram = nc.dram_tensor("bc_dram", [2 * N, L], f32).ap()
        x1_dram = nc.dram_tensor("x1_dram", [P, KD, L], f32).ap()

        ring = {f"{c}{k}": sb(f"w_{c}{k}", [P, 4, L]) for c in "gud" for k in range(2)}
        wdt = sb("wdt", [P, KE, DT])
        wbc = sb("wbc", [P, KE, 2 * N])
        wd2 = sb("wd2", [P, E])
        small = sb("small", [P, SMALL])
        aneg = sb("aneg_ready", [P, KE, N])
        ones = sb("ones", [P, P])
        X = {"F": sb("res_f", [P, KD, L]), "G": sb("res_g", [P, KD, L])}
        z = sb("normed_ready", [P, KD, L])
        zm = sb("zm", [P, KD, L])
        rt = sb("rt", [P, L])
        rs = sb("rs", [P, L])
        h = [sb(f"h{k}", [P, 4, L]) for k in range(2)]
        ab = sb("ab", [P, 4, L])
        cmp = sb("cmp", [P, 6, L], bf16)
        part = sb("part", [P, 4, L], bf16)
        wins = sb("wins", [P, 4, L], bf16)
        sg = [sb(f"sg{k}", [P, L]) for k in range(2)]
        y = sb("y", [P, KE, L])
        delta = sb("delta", [P, KE, L])
        du = sb("du", [P, KE, L])
        Bb = [sb(f"Bb{k}", [P, L]) for k in range(2)]
        Cb = [sb(f"Cb{k}", [P, L]) for k in range(2)]
        up = [sb(f"up{k}", [P, DC - 1 + L]) for k in range(2)]
        db = [u[:, DC - 1:] for u in up]
        hs = [sb(f"hs{k}", [P, L]) for k in range(2)]
        pr = [sb(f"pr{k}", [P, L]) for k in range(2)]
        bcs = pr[0][0:2 * N, :]
        dts = hs[0]
        cv = sg

        gu = [pb(f"gu{b}") for b in range(4)]
        dn = [pb(f"dn{b}") for b in range(2)]
        pa = [pb(f"pa{b}") for b in range(2)]

        sem = {}
        names = ["params_loaded", "const_ready", "aneg_ready"] + list(PER)
        for name in names:
            sem[name] = ctx.enter_context(nc.semaphore("s_" + name))
        INIT_DMAS = 4

        block = ctx.enter_context(nc.Block())

        def over(eng, walk, body, peel):
            peel("prologue")
            body(FULL[:0] + [None] * 4 + ["G"] * 4, True, True, None, 0)
            with eng.Fori(0, B - 2) as i:
                walk.enter(i, PER)
                body(FULL, True, True, i, 1)
                walk.leave(B - 2)
            body(["F"] * 4 + [None] * 4, True, False, None, B - 1)
            peel("epilogue")

        @block.sync
        def _(sp):
            w = Walk()
            for dst, src in ((small[:], small_in), (wdt[:], wdt_in), (wbc[:], wbc_in), (wd2[:], wd2_in)):
                sp.dma_start(dst, src).then_inc(sem["params_loaded"], 16)

            def load(slot, src):
                sp.dma_start(ring[slot][:], src).then_inc(sem["loaded_" + slot], 16)
                w.add("loaded_" + slot, 16)

            def body(kinds, outp, proj, i, b, scan=True, before=(17, 10)):
                g0, d0, u0 = w.count("product_ready"), w.count("down_ready"), w.count("weighted_ready")
                bcst = w.count("bc_stored")
                order = dn_order(kinds)
                k_of = {s: k for k, s in enumerate(s for s, kd in enumerate(kinds) if kd)}
                if "G" in kinds and scan:
                    sp.wait_ge(sem["normed_ready"], w.at("normed_ready"))
                    sp.wait_ge(sem["x1_stored"], w.at("x1_stored"))
                    nb = (i + (b + 1)) if i is not None else b + 1
                    sp.dma_start(X["G"][:], x_in[bass.ds(nb, 1)].rearrange("o p k t -> (o p) k t")).then_inc(sem["x_loaded"], 16)
                    w.add("x_loaded", 16)

                def gate_up(s):
                    if s >= len(kinds) or not kinds[s]:
                        return
                    for c, which, last in (("g", 0, 7), ("u", 1, 8)):
                        if k_of[s] >= 2:
                            sp.wait_ge(sem["product_ready"], w.at("product_ready", g0 + 8 * (k_of[s] - 2) + last))
                        else:
                            sp.wait_ge(sem["product_ready"], w.at("product_ready", g0 - before[s % 2]))
                        load(f"{c}{s % 2}", ffn_w[s % 4, which])

                def down(s):
                    if s >= len(kinds) or not kinds[s]:
                        return
                    if k_of[s] >= 2:
                        sp.wait_ge(sem["down_ready"], w.at("down_ready", d0 + order.index(("down", s - 2, KD - 1)) + 1))
                    else:
                        sp.wait_ge(sem["product_ready"], w.at("product_ready", g0 - before[0]))
                    load(f"d{s % 2}", ffn_w[s % 4, 2])

                def spread(n):
                    if not scan or n >= N:
                        return
                    if n < 2:
                        sp.wait_ge(sem["bc_stored"], w.at("bc_stored", bcst))
                    else:
                        sp.wait_ge(sem["weighted_ready"], w.at("weighted_ready", u0 + KE * (n - 1)))
                    for dst, row in ((Bb[n % 2], n), (Cb[n % 2], N + n)):
                        sp.dma_start(dst[:], bc_dram[row:row + 1, :].broadcast_to([P, L])).then_inc(sem[f"bc_loaded_{n % 2}"], 16)
                    w.add(f"bc_loaded_{n % 2}", 32)

                spread(0)
                spread(1)
                gate_up(0)
                gate_up(1)
                down(0)
                for s in range(len(kinds)):
                    spread(2 * s + 2)
                    spread(2 * s + 3)
                    gate_up(s + 2)
                    down(s + 1)
                    if s == 5 and kinds[0]:
                        store_out(b, i, d0 + order.index(("down", 3, KD - 1)) + 1)
                    if s == 6 and outp:
                        if kinds[0]:
                            sp.wait_ge(sem["out_stored"], w.at("out_stored"))
                        sp.wait_ge(sem["x1_stored"], w.at("x1_stored"))
                        sp.dma_start(X["F"][:], x1_dram).then_inc(sem["x1_loaded"], 16)
                        w.add("x1_loaded", 16)
                w.add("product_ready", 8 * len(k_of))
                w.add("bank_read_1", 2 * len(k_of))
                w.add("down_ready", len(order))
                w.add("weighted_ready", UNITS if scan else 0)

                gu1, dn1 = g0 + 8 * len(k_of), d0 + len(order)
                if outp:
                    for slot, n, left in (("g0", 2, 9), ("u0", 3, 8)):
                        sp.wait_ge(sem["product_ready"], w.at("product_ready", gu1 - left))
                        load(slot, mam_w[n])
                    for slot, n, left in (("d0", 4, KD), ("d1", 5, 0)):
                        sp.wait_ge(sem["down_ready"], w.at("down_ready", dn1 - left))
                        load(slot, mam_w[n])
                if proj:
                    for slot, n, left in (("g1", 0, 1), ("u1", 1, 0)):
                        sp.wait_ge(sem["product_ready"], w.at("product_ready", gu1 - left))
                        load(slot, mam_w[n])
                tail(outp, proj, kinds[-1] == "G")

            def store_out(b, i, done):
                sp.wait_ge(sem["down_read"], w.at("down_read", done))
                ob = (i + (b - 1)) if i is not None else b - 1
                sp.dma_start(out[bass.ds(ob, 1)].rearrange("o p k t -> (o p) k t"), X["F"][:]).then_inc(sem["out_stored"], 16)
                w.add("out_stored", 16)

            def tail(outp, proj, ffn1):
                if outp:
                    w.add("product_ready", OUTP_JOBS)
                    w.add("bank_read_1", BANK_SK.count(1) + BANK_OUT.count(1))
                if proj:
                    if ffn1:
                        sp.wait_ge(sem["down_read"], w.at("down_read", w.count("down_ready")))
                    sp.dma_start(x1_dram, X["G"][:]).then_inc(sem["x1_stored"], 16)
                    w.add("x1_stored", 16)
                    w.add("down_ready", 2)
                    w.add("bank_read_1", BANK_IN.count(1) + 1)
                    sp.wait_ge(sem["bank_read_1"], w.at("bank_read_1"))
                    w.add("bank_read_1", BANK_DL.count(1))
                    sp.dma_start(bc_dram, bcs).then_inc(sem["bc_stored"], 16)
                    w.add("bc_stored", 16)
                    w.add("product_ready", PROJ_JOBS)
                    w.add("normed_ready")
                w.add("down_read", w.count("down_ready") - w.count("down_read"))

            def body_z(kinds, outp, proj, i, b, scan=True, before=(17, 10)):
                body(kinds, outp, proj, i, b, scan, before)
                w.add("normed_ready", sum(kd is not None for kd in kinds[::4]))

            def peel(part):
                if part == "prologue":
                    sp.dma_start(X["G"][:], x_in[0]).then_inc(sem["x_loaded"], 16)
                    w.add("x_loaded", 16)
                    body_z(["G"] * 4, False, True, None, -1, scan=False, before=(0, 0))
                else:
                    body_z(["F"] * 4, False, False, None, B, scan=False, before=(0, 0))
                    store_out(B, None, w.count("down_read"))
                    for name in ("out_stored", "x1_stored", "bc_stored"):
                        sp.wait_ge(sem[name], w.at(name))

            over(sp, w, body_z, peel)

        @block.tensor
        def _(pe):
            w = Walk()

            def weights(slot):
                w.add("loaded_" + slot, 16)
                pe.wait_ge(sem["loaded_" + slot], w.at("loaded_" + slot))

            def job(bank, pairs, rows=P):
                pe.wait_ge(sem[f"bank_read_{bank}"], w.at(f"bank_read_{bank}"))
                w.add(f"bank_read_{bank}")
                for k, (lhsT, rhs) in enumerate(pairs):
                    mm = nc.tensor.matmul(gu[bank][0:rows, :], lhsT, rhs, start=(k == 0), stop=(k == len(pairs) - 1))
                mm.then_inc(sem["product_ready"], 1)
                w.add("product_ready")

            def dn_job(pairs):
                k = w.count("down_ready")
                pe.wait_ge(sem["down_read"], w.at("down_read", k - 1))
                for m, (lhsT, rhs) in enumerate(pairs):
                    mm = nc.tensor.matmul(dn[k % 2][:], lhsT, rhs, start=(m == 0), stop=(m == len(pairs) - 1))
                mm.then_inc(sem["down_ready"], 1)
                w.add("down_ready")

            def norm(x):
                dn_job([(ones[:], x[:, k, :]) for k in range(KD)])
                w.add("squares_ready")
                pe.wait_ge(sem["squares_ready"], w.at("squares_ready"))
                dn_job([(ones[:], h[0][:, k, :]) for k in range(KD)])
                w.add("normed_ready")

            def body(kinds, outp, proj, i, b, scan=True):
                if kinds[0] == "F":
                    for t in range(KD):
                        pe.wait_ge(sem[f"bank_read_{BANK_OUT[t]}"], w.at(f"bank_read_{BANK_OUT[t]}"))
                if "G" in kinds:
                    w.add("x_loaded", 16)
                for s, kind in enumerate(kinds):
                    if kind and s % 4 == 0:
                        if kind == "G":
                            pe.wait_ge(sem["x_loaded"], w.at("x_loaded"))
                        norm(X[kind])
                        pe.wait_ge(sem["normed_ready"], w.at("normed_ready"))
                    for j in range(4):
                        if kind:
                            for c, side in (("g", 0), ("u", 1)):
                                slot = f"{c}{s % 2}"
                                if j == 0:
                                    weights(slot)
                                wt = ring[slot][:].rearrange("p k (j m) -> p k j m", j=4)
                                job(2 * (j % 2) + side, [(wt[:, k, j, :], z[:, k, :]) for k in range(KD)])
                        if j >= 2 and s > 0 and kinds[s - 1]:
                            downs(s - 1, range(2 * (j - 2), 2 * (j - 1)))
                if kinds[-1]:
                    downs(len(kinds) - 1, range(KD))
                tail(outp, proj)

            def downs(s, ts):
                if ts[0] == 0:
                    weights(f"d{s % 2}")
                    w.add("hidden_ready")
                    pe.wait_ge(sem["hidden_ready"], w.at("hidden_ready"))
                wt = ring[f"d{s % 2}"]
                for t in ts:
                    dn_job([(wt[:, j, t * P:(t + 1) * P], h[s % 2][:, j, :]) for j in range(4)])

            def tail(outp, proj):
                if outp:
                    for e in range(KE):
                        slot = ("g0", "u0")[e // 4]
                        if e % 4 == 0:
                            weights(slot)
                        o = (e % 4) * P
                        job(BANK_SK[e], [(ring[slot][:, k, o:o + P], zm[:, k, :]) for k in range(KD)])
                    weights("d0")
                    weights("d1")
                    w.add("gated_ready", KE)
                    pe.wait_ge(sem["gated_ready"], w.at("gated_ready"))
                    for t in range(KD):
                        job(BANK_OUT[t], [(ring[("d0", "d1")[e // 4]][:, e % 4, t * P:(t + 1) * P], y[:, e, :])
                                          for e in range(KE)])
                if proj:
                    pe.wait_ge(sem["down_read"], w.at("down_read", w.count("down_ready")))
                    norm(X["G"])
                    pe.wait_ge(sem["normed_ready"], w.at("normed_ready"))
                    for e in range(KE):
                        slot = ("g1", "u1")[e // 4]
                        if e % 4 == 0:
                            weights(slot)
                        o = (e % 4) * P
                        job(BANK_IN[e], [(ring[slot][:, k, o:o + P], zm[:, k, :]) for k in range(KD)])
                    w.add("u_ready", KE)
                    pe.wait_ge(sem["u_ready"], w.at("u_ready"))
                    job(BANK_DT, [(wdt[:, e, :], y[:, e, :]) for e in range(KE)])
                    job(BANK_BC, [(wbc[:, e, :], y[:, e, :]) for e in range(KE)], rows=2 * N)
                    pe.wait_ge(sem[f"bank_read_{BANK_DT}"], w.at(f"bank_read_{BANK_DT}"))
                    for e in range(KE):
                        job(BANK_DL[e], [(wd2[:, e * P:(e + 1) * P], dts[:])])
                w.add("down_read", w.count("down_ready") - w.count("down_read"))

            def peel(part):
                if part == "prologue":
                    pe.wait_ge(sem["params_loaded"], 16 * INIT_DMAS)
                    pe.wait_ge(sem["const_ready"], 1)
                    body(["G"] * 4, False, True, None, -1)
                else:
                    body(["F"] * 4, False, False, None, B)

            over(pe, w, body, peel)

        @block.scalar
        def _(act):
            w = Walk()

            def squares(mean, src):
                act.wait_ge(sem["down_read"], w.at("down_read", mean + 1))
                nc.scalar.activation(h[0][:], src[:], ACT.Square).then_inc(sem["squares_ready"], 1)

            def root():
                nc.scalar.activation(rt[:], rt[:], ACT.Sqrt).then_inc(sem["root_ready"], 1)

            def silu(s, j):
                gate, upb = 2 * (j % 2), 2 * (j % 2) + 1
                w.add("product_ready")
                act.wait_ge(sem["product_ready"], w.at("product_ready"))
                act.wait_ge(sem[f"bank_read_{upb}"], w.at(f"bank_read_{upb}"))
                nc.scalar.activation(sg[j % 2][:], gu[gate][:], ACT.Silu).then_inc(sem[f"bank_read_{gate}"], 1)
                w.add(f"bank_read_{gate}")
                w.add("product_ready")
                w.add(f"bank_read_{upb}")

            def absolute(s, j):
                upb = 2 * (j % 2) + 1
                act.wait_ge(sem[f"bank_read_{upb}"], w.at(f"bank_read_{upb}"))
                if j == 0:
                    act.wait_ge(sem["hidden_ready"], w.at("hidden_ready"))
                nc.scalar.activation(ab[:, j, :], h[s % 2][:, j, :], ACT.Abs).then_inc(sem["magnitude_ready"], 1)
                if j == 3:
                    w.add("hidden_ready")

            def decay(u):
                n, e = u // KE, u % KE
                act.wait_ge(sem["state_ready"], w.at("state_ready", w.count("state_ready") + u - 1))
                nc.scalar.activation(pa[u % 2][:], delta[:, e, :], ACT.Exp, scale=aneg[:, e, n:n + 1]).then_inc(sem["decay_ready"], 1)

            def body(kinds, outp, proj, i, b, scan=True):
                if scan:
                    act.wait_ge(sem["delta_ready"], w.at("delta_ready"))
                dn0 = w.count("down_ready")
                order = dn_order(kinds)
                slots = [(s, j) for s in range(len(kinds)) for j in range(4)]
                for m, (s, j) in enumerate(slots):
                    prev = slots[m - 1] if m and kinds[slots[m - 1][0]] else None
                    if prev:
                        silu(*prev)
                    if j == 0 and kinds[s] and s % 4 == 0:
                        mean = dn0 + order.index(("norm", s, 0))
                        squares(mean, z)
                        act.wait_ge(sem["down_read"], w.at("down_read", mean + 2))
                        root()
                    if scan:
                        for u in range(4 * m, 4 * m + 4):
                            decay(u)
                    if prev:
                        absolute(*prev)
                if kinds[-1]:
                    silu(*slots[-1])
                    absolute(*slots[-1])
                w.add("down_ready", len(order))
                if scan:
                    w.add("state_ready", UNITS)
                tail(outp, proj)
                w.add("down_read", w.count("down_ready") - w.count("down_read"))

            def tail(outp, proj):
                if outp:
                    for e in range(KE):
                        w.add("product_ready")
                        act.wait_ge(sem["product_ready"], w.at("product_ready"))
                        act.wait_ge(sem["gated_ready"], w.at("gated_ready", w.count("gated_ready") + e - 1))
                        nc.scalar.activation(sg[e % 2][:], gu[BANK_SK[e]][:], ACT.Silu).then_inc(sem[f"bank_read_{BANK_SK[e]}"], 1)
                        w.add(f"bank_read_{BANK_SK[e]}")
                    w.add("gated_ready", KE)
                    for t in range(KD):
                        w.add("product_ready")
                        w.add(f"bank_read_{BANK_OUT[t]}")
                if proj:
                    squares(w.count("down_ready"), zm)
                    w.add("down_ready", 2)
                    for _ in range(2):
                        w.add("variance_ready")
                        act.wait_ge(sem["variance_ready"], w.at("variance_ready"))
                        root()

                    def conv_silu(e):
                        act.wait_ge(sem["conv_ready"], w.at("conv_ready", w.count("conv_ready") + e + 1))
                        nc.scalar.activation(y[:, e, :], cv[e % 2][:], ACT.Silu).then_inc(sem["u_ready"], 1)

                    for e in range(KE):
                        w.add("product_ready")
                        act.wait_ge(sem["product_ready"], w.at("product_ready"))
                        act.wait_ge(sem["conv_ready"], w.at("conv_ready", w.count("conv_ready") + e - 1))
                        nc.scalar.activation(up[e % 2][:, DC - 1:], gu[BANK_IN[e]][:], ACT.Copy).then_inc(sem[f"bank_read_{BANK_IN[e]}"], 1)
                        w.add(f"bank_read_{BANK_IN[e]}")
                        if e:
                            conv_silu(e - 1)
                    conv_silu(KE - 1)
                    w.add("conv_ready", KE)
                    w.add("product_ready")
                    act.wait_ge(sem["product_ready"], w.at("product_ready"))
                    nc.scalar.activation(dts[:], gu[BANK_DT][:], ACT.Copy).then_inc(sem[f"bank_read_{BANK_DT}"], 1)
                    w.add(f"bank_read_{BANK_DT}")
                    w.add("product_ready")
                    act.wait_ge(sem["product_ready"], w.at("product_ready"))
                    act.wait_ge(sem["bc_stored"], w.at("bc_stored"))
                    nc.scalar.activation(bcs, gu[BANK_BC][0:2 * N, :], ACT.Copy).then_inc(sem[f"bank_read_{BANK_BC}"], 1)
                    w.add(f"bank_read_{BANK_BC}")
                    w.add("bc_stored", 16)
                    for e in range(KE):
                        w.add("product_ready")
                        act.wait_ge(sem["product_ready"], w.at("product_ready"))
                        nc.scalar.activation(du[:, e, :], gu[BANK_DL[e]][:], ACT.Identity,
                                             bias=small[:, C_BD + e:C_BD + e + 1]).then_inc(sem[f"bank_read_{BANK_DL[e]}"], 1)
                        w.add(f"bank_read_{BANK_DL[e]}")
                    for b in (BANK_DL[KE - 2], BANK_DL[KE - 1], BANK_DL[KE - 4], BANK_DL[KE - 3]):
                        act.wait_ge(sem[f"bank_read_{b}"], w.at(f"bank_read_{b}"))
                    nc.scalar.activation(delta[:], du[:], ACT.Abs).then_inc(sem["act_step"], 1)
                    w.add("act_step")
                    act.wait_ge(sem["act_step"], w.at("act_step"))
                    nc.scalar.activation(delta[:], delta[:], ACT.Exp, scale=-1.0).then_inc(sem["act_step"], 1)
                    w.add("act_step")
                    act.wait_ge(sem["act_step"], w.at("act_step"))
                    for half in range(2):
                        es = slice(half * KE // 2, (half + 1) * KE // 2)
                        nc.scalar.activation(delta[:, es, :], delta[:, es, :], ACT.Ln, bias=1.0).then_inc(sem["log_ready"], 1)
                    w.add("log_ready", 2)
                    w.add("delta_ready", 2)

            def peel(part):
                if part == "prologue":
                    act.wait_ge(sem["params_loaded"], 16 * INIT_DMAS)
                    nc.scalar.activation(aneg[:], small[:, C_AL:C_AL + KE * N].rearrange("p (e n) -> p e n", n=N),
                                         ACT.Exp).then_inc(sem["aneg_ready"], 1)
                    act.wait_ge(sem["aneg_ready"], 1)
                    nc.scalar.mul(aneg[:], aneg[:], -1.0).then_inc(sem["aneg_ready"], 1)
                    act.wait_ge(sem["aneg_ready"], 2)
                    body(["G"] * 4, False, True, None, -1, scan=False)
                else:
                    body(["F"] * 4, False, False, None, B, scan=False)

            over(act, w, body, peel)

        @block.vector
        def _(dve):
            w = Walk()

            def own(ins):
                ins.then_inc(sem["dve_step"], 1)
                w.add("dve_step")
                dve.wait_ge(sem["dve_step"], w.at("dve_step"))

            def centre(x, dst):
                k = w.count("down_ready")
                w.add("down_ready")
                dve.wait_ge(sem["down_ready"], w.at("down_ready", k + 1))
                nc.vector.tensor_tensor(dst[:], x[:], dn[k % 2][:].unsqueeze(1).broadcast_to([P, KD, L]),
                                        ALU.subtract).then_inc(sem["down_read"], 1)

            def root_of(count):
                w.add("root_ready")
                dve.wait_ge(sem["root_ready"], w.at("root_ready"))

            def norm_ffn(x):
                centre(x, z)
                k = w.count("down_ready")
                w.add("down_ready")
                dve.wait_ge(sem["down_ready"], w.at("down_ready", k + 1))
                nc.vector.tensor_scalar(rt[:], dn[k % 2][:], EPS, None, ALU.add).then_inc(sem["down_read"], 1)
                root_of(1)
                own(nc.vector.reciprocal(rs[:], rt[:]))
                nc.vector.tensor_tensor(z[:], z[:], rs[:].unsqueeze(1).broadcast_to([P, KD, L]),
                                        ALU.mult).then_inc(sem["normed_ready"], 1)

            def norm_mamba(x):
                centre(x, zm)
                k = w.count("down_ready")
                w.add("down_ready")
                dve.wait_ge(sem["down_ready"], w.at("down_ready", k + 1))
                nc.vector.tensor_scalar(rt[:], dn[k % 2][:], EPS, None, ALU.add).then_inc(sem["variance_ready"], 1)
                root_of(1)
                own(nc.vector.reciprocal(rs[:], rt[:]))
                own(nc.vector.tensor_tensor(rt[:], rs[:], rs[:], ALU.mult))
                nc.vector.tensor_tensor(rt[:], rt[:], dn[k % 2][:], ALU.mult).then_inc(sem["down_read"], 1)
                dve.wait_ge(sem["down_read"], w.at("down_read", k + 1))
                nc.vector.tensor_scalar(rt[:], rt[:], EPS, None, ALU.add).then_inc(sem["variance_ready"], 1)
                root_of(2)
                own(nc.vector.reciprocal(rt[:], rt[:]))
                own(nc.vector.tensor_tensor(rs[:], rs[:], rt[:], ALU.mult))
                for k in range(KD):
                    last = nc.vector.scalar_tensor_tensor(zm[:, k, :], zm[:, k, :], small[:, C_NORM + k:C_NORM + k + 1],
                                                          rs[:], ALU.mult, ALU.mult)
                last.then_inc(sem["normed_ready"], 1)

            def pair(s, j):
                gate, upb = 2 * (j % 2), 2 * (j % 2) + 1
                w.add("product_ready", 2)
                w.add(f"bank_read_{gate}")
                dve.wait_ge(sem["product_ready"], w.at("product_ready"))
                dve.wait_ge(sem[f"bank_read_{gate}"], w.at(f"bank_read_{gate}"))
                nc.vector.tensor_tensor(h[s % 2][:, j, :], gu[upb][:], sg[j % 2][:], ALU.mult).then_inc(sem[f"bank_read_{upb}"], 1)
                w.add(f"bank_read_{upb}")

            def sparsify(s):
                w.add("magnitude_ready", 4)
                dve.wait_ge(sem["magnitude_ready"], w.at("magnitude_ready"))
                dve.wait_ge(sem["hidden_ready"], w.at("hidden_ready"))
                for i, first in ((0, 0), (1, 3), (2, 5)):
                    m = 3 - i
                    last = nc.vector.tensor_tensor(cmp[:, first:first + m, :],
                                                   ab[:, i:i + 1, :].broadcast_to([P, m, L]), ab[:, i + 1:4, :], ALU.is_ge)
                own(last)
                nc.vector.tensor_tensor(part[:, 0:2, :], cmp[:, 1:4:2, :], cmp[:, 2:5:2, :], ALU.add)
                own(nc.vector.tensor_tensor(part[:, 2:4, :], cmp[:, 1:3, :], cmp[:, 3:5, :], ALU.add))
                nc.vector.tensor_tensor(wins[:, 0, :], part[:, 0, :], cmp[:, 0, :], ALU.add)
                nc.vector.tensor_tensor(wins[:, 1, :], part[:, 1, :], cmp[:, 0, :], ALU.subtract)
                nc.vector.tensor_tensor(wins[:, 2, :], cmp[:, 5, :], part[:, 2, :], ALU.subtract)
                own(nc.vector.tensor_tensor(wins[:, 3, :], cmp[:, 5, :], part[:, 3, :], ALU.add))
                for i, (op, least) in enumerate(((ALU.is_ge, 2.0), (ALU.is_ge, 1.0), (ALU.is_ge, 0.0), (ALU.is_le, 1.0))):
                    last = nc.vector.scalar_tensor_tensor(h[s % 2][:, i, :], wins[:, i, :], least, h[s % 2][:, i, :], op, ALU.mult)
                last.then_inc(sem["hidden_ready"], 1)
                w.add("hidden_ready")

            def add_down(kind, ts):
                for t in ts:
                    k = w.count("down_ready")
                    w.add("down_ready")
                    dve.wait_ge(sem["down_read"], w.at("down_read", k))
                    dve.wait_ge(sem["down_ready"], w.at("down_ready", k + 1))
                    nc.vector.scalar_tensor_tensor(X[kind][:, t, :], dn[k % 2][:], 0.5, X[kind][:, t, :],
                                                   ALU.mult, ALU.add).then_inc(sem["down_read"], 1)

            def scan(u0, u):
                dve.wait_ge(sem["decay_ready"], w.at("decay_ready", u0 + u + 1))
                dve.wait_ge(sem["input_ready"], w.at("input_ready", u0 + u + 1))
                dve.wait_ge(sem["weighted_ready"], w.at("weighted_ready", u0 + u - 1))
                nc.vector.tensor_tensor_scan(hs[u % 2][:], pa[u % 2][:], db[u % 2], 0.0, ALU.mult,
                                             ALU.add).then_inc(sem["state_ready"], 1)

            def times_c(u0, u):
                n, e = u // KE, u % KE
                if e == 0:
                    w.add(f"bc_loaded_{n % 2}", 32)
                    dve.wait_ge(sem[f"bc_loaded_{n % 2}"], w.at(f"bc_loaded_{n % 2}"))
                dve.wait_ge(sem["state_ready"], w.at("state_ready", u0 + u + 1))
                dve.wait_ge(sem["sum_ready"], w.at("sum_ready", u0 + u - 1))
                nc.vector.tensor_tensor(pr[u % 2][:], hs[u % 2][:], Cb[n % 2][:], ALU.mult).then_inc(sem["weighted_ready"], 1)

            def body(kinds, outp, proj, i, b, with_scan=True):
                u0 = w.count("state_ready")
                S = len(kinds)
                slots = [(s, j) for s in range(S) for j in range(4)]
                for m, (s, j) in enumerate(slots):
                    if j == 3 and s > 0 and kinds[s - 1]:
                        add_down(kinds[s - 1], (0, 1))
                    if j == 0 and s > 1 and kinds[s - 2]:
                        add_down(kinds[s - 2], (2, 3))
                    prev = slots[m - 1] if m and kinds[slots[m - 1][0]] else None
                    if prev:
                        pair(*prev)
                    if j == 0 and kinds[s] and s % 4 == 0:
                        norm_ffn(X[kinds[s]])
                    if with_scan:
                        for u in range(4 * m, 4 * m + 4):
                            scan(u0, u)
                            if u:
                                times_c(u0, u - 1)
                    if prev and prev[1] == 3:
                        sparsify(prev[0])
                if with_scan:
                    times_c(u0, UNITS - 1)
                    for name in ("state_ready", "decay_ready", "input_ready", "weighted_ready", "sum_ready"):
                        w.add(name, UNITS)
                if kinds[-1]:
                    add_down(kinds[-1], (2, 3))
                    pair(*slots[-1])
                    sparsify(S - 1)
                    add_down(kinds[-1], range(KD))
                tail(outp, proj)
                w.add("down_read", w.count("down_ready") - w.count("down_read"))

            def tail(outp, proj):
                if outp:
                    dve.wait_ge(sem["sum_ready"], w.at("sum_ready"))
                    for e in range(KE):
                        w.add("product_ready")
                        w.add(f"bank_read_{BANK_SK[e]}")
                        dve.wait_ge(sem[f"bank_read_{BANK_SK[e]}"], w.at(f"bank_read_{BANK_SK[e]}"))
                        nc.vector.tensor_tensor(y[:, e, :], y[:, e, :], sg[e % 2][:], ALU.mult).then_inc(sem["gated_ready"], 1)
                    w.add("gated_ready", KE)
                    w.add("x1_loaded", 16)
                    dve.wait_ge(sem["x1_loaded"], w.at("x1_loaded"))
                    for t in range(KD):
                        w.add("product_ready")
                        dve.wait_ge(sem["product_ready"], w.at("product_ready"))
                        bank = BANK_OUT[t]
                        nc.vector.tensor_tensor(X["F"][:, t, :], gu[bank][:], X["F"][:, t, :], ALU.add).then_inc(sem[f"bank_read_{bank}"], 1)
                        w.add(f"bank_read_{bank}")
                if proj:
                    dve.wait_ge(sem["down_read"], w.at("down_read", w.count("down_ready")))
                    norm_mamba(X["G"])
                    for e in range(KE):
                        w.add("product_ready")
                        w.add(f"bank_read_{BANK_IN[e]}")
                        dve.wait_ge(sem[f"bank_read_{BANK_IN[e]}"], w.at(f"bank_read_{BANK_IN[e]}"))
                        dve.wait_ge(sem["u_ready"], w.at("u_ready", w.count("u_ready") + e - 1))
                        c, x = cv[e % 2], up[e % 2]
                        tap = lambda k: small[:, C_CW + e * DC + k:C_CW + e * DC + k + 1]
                        own(nc.vector.tensor_scalar(c[:], x[:, 0:L], tap(0), small[:, C_CB + e:C_CB + e + 1], ALU.mult, ALU.add))
                        for k in range(1, DC):
                            ins = nc.vector.scalar_tensor_tensor(c[:], x[:, k:k + L], tap(k), c[:], ALU.mult, ALU.add)
                            if k < DC - 1:
                                own(ins)
                        ins.then_inc(sem["conv_ready"], 1)
                    w.add("u_ready", KE)
                    w.add("product_ready", 2 + KE)
                    for bank in [BANK_DT, BANK_BC] + BANK_DL:
                        w.add(f"bank_read_{bank}")
                    for half in range(2):
                        es = slice(half * KE // 2, (half + 1) * KE // 2)
                        w.add("log_ready")
                        dve.wait_ge(sem["log_ready"], w.at("log_ready"))
                        nc.vector.scalar_tensor_tensor(delta[:, es, :], du[:, es, :], 0.0, delta[:, es, :],
                                                       ALU.max, ALU.add).then_inc(sem["delta_ready"], 1)
                        w.add("delta_ready")
                        dve.wait_ge(sem["delta_ready"], w.at("delta_ready"))
                        own(nc.vector.tensor_tensor(du[:, es, :], delta[:, es, :], y[:, es, :], ALU.mult))
                        for e in range(es.start, es.stop):
                            last = nc.vector.tensor_scalar(y[:, e, :], y[:, e, :], small[:, C_WD + e:C_WD + e + 1], None, ALU.mult)
                        last.then_inc(sem["first_term_ready"], 1)

            def peel(part):
                if part == "prologue":
                    dve.wait_ge(sem["params_loaded"], 16 * INIT_DMAS)
                    dve.wait_ge(sem["const_ready"], 3)
                    body(["G"] * 4, False, True, None, -1, with_scan=False)
                else:
                    body(["F"] * 4, False, False, None, B, with_scan=False)

            over(dve, w, body, peel)

        @block.gpsimd
        def _(pool):
            w = Walk()

            def input_of(u0, u):
                n, e = u // KE, u % KE
                if e == 0:
                    w.add(f"bc_loaded_{n % 2}", 32)
                    pool.wait_ge(sem[f"bc_loaded_{n % 2}"], w.at(f"bc_loaded_{n % 2}"))
                pool.wait_ge(sem["state_ready"], w.at("state_ready", u0 + u - 1))
                nc.gpsimd.tensor_tensor(db[u % 2], du[:, e, :], Bb[n % 2][:], ALU.mult).then_inc(sem["input_ready"], 1)

            def sum_states(u0, u):
                e = u % KE
                pool.wait_ge(sem["weighted_ready"], w.at("weighted_ready", u0 + u + 1))
                pool.wait_ge(sem["sum_ready"], w.at("sum_ready", u0 + u - KE + 1))
                nc.gpsimd.tensor_tensor(y[:, e, :], y[:, e, :], pr[u % 2][:], ALU.add).then_inc(sem["sum_ready"], 1)

            def body(kinds, outp, proj, i, b):
                u0 = w.count("state_ready")
                w.add("first_term_ready", 2)
                pool.wait_ge(sem["first_term_ready"], w.at("first_term_ready"))
                for u in range(UNITS):
                    input_of(u0, u)
                    if u >= 2:
                        sum_states(u0, u - 2)
                for u in range(UNITS - 2, UNITS):
                    sum_states(u0, u)
                for name in ("state_ready", "weighted_ready", "sum_ready"):
                    w.add(name, UNITS)

            def peel(part):
                if part == "prologue":
                    nc.gpsimd.memset(ones[:], 1.0 / D).then_inc(sem["const_ready"], 1)
                    for k in range(2):
                        nc.gpsimd.memset(up[k][:, 0:DC - 1], 0.0).then_inc(sem["const_ready"], 1)

            over(pool, w, body, peel)


_ORDER = ["x_in", "ffn_w", "mam_w", "wdt_in", "wbc_in", "wd2_in", "small_in"]


def _tiles(v):
    return v.reshape(-1, P).T


def kernel(L0_attn_x, L0_attn_norm_w, L0_attn_W_skip, L0_attn_W_in, L0_attn_conv_w, L0_attn_conv_b, L0_attn_Wd1,
           L0_attn_Wd2, L0_attn_bd2, L0_attn_WB, L0_attn_WC, L0_attn_A_log, L0_attn_W_D, L0_attn_W_out,
           L0_ffn_w_gate, L0_ffn_w_up, L0_ffn_w_down):
    import concourse.bacc as bacc
    from concourse.bass_utils import run_bass_kernel_spmd

    a = np.asarray
    x = a(L0_attn_x).transpose(0, 2, 1).reshape(B, KD, P, L).transpose(0, 2, 1, 3)
    cols = lambda v: a(v).reshape(KD, P, QUADS, P, 4).transpose(2, 1, 0, 4, 3).reshape(QUADS, P, 4, L)
    down = a(L0_ffn_w_down).reshape(QUADS, P, 4, D)
    ffn = np.stack([cols(L0_ffn_w_gate), cols(L0_ffn_w_up), down], axis=1)
    inner = lambda v: a(v).T.reshape(KD, P, 2, E // 2).transpose(2, 1, 0, 3)
    outer = a(L0_attn_W_out).T.reshape(2, 4, P, D).transpose(0, 2, 1, 3)
    mam = np.concatenate([inner(L0_attn_W_in), inner(L0_attn_W_skip), outer])
    over_e = lambda v: a(v).T.reshape(KE, P, -1).transpose(1, 0, 2)
    wbc = over_e(np.concatenate([a(L0_attn_WB), a(L0_attn_WC)]))
    per_e = lambda v: a(v).reshape(KE, P, -1).transpose(1, 0, 2).reshape(P, -1)
    small = np.concatenate([_tiles(a(L0_attn_norm_w)), per_e(L0_attn_conv_w), _tiles(a(L0_attn_conv_b)),
                            _tiles(a(L0_attn_bd2)), per_e(L0_attn_A_log), _tiles(a(L0_attn_W_D))], axis=1)
    arrays = {"x_in": x, "ffn_w": ffn, "mam_w": mam, "wdt_in": over_e(L0_attn_Wd1), "wbc_in": wbc,
              "wd2_in": a(L0_attn_Wd2).T, "small_in": small}
    arrays = {k: np.ascontiguousarray(v) for k, v in arrays.items()}

    nc = bacc.Bacc("TRN2", target_bir_lowering=False, num_devices=1)
    args = {k: nc.dram_tensor(k + "_dram", v.shape, mybir.dt.from_np(v.dtype), kind="ExternalInput").ap()
            for k, v in arrays.items()}
    out = nc.dram_tensor("out_dram", (B, P, KD, L), mybir.dt.float32, kind="ExternalOutput").ap()
    build(nc, out=out, **args)
    r = run_bass_kernel_spmd(nc, [{k + "_dram": v for k, v in arrays.items()}], core_ids=[0])
    got = r.results[0]["out_dram"]
    return np.ascontiguousarray(got.transpose(0, 2, 1, 3).reshape(B, D, L).transpose(0, 2, 1))
```

```python
import numpy as np
import concourse.bass as bass
from concourse import mybir
from contextlib import ExitStack


B, L, D = 8, 512, 512
E, N, DT, DC = 1024, 16, 128, 4
I = 2048
P = 128
KD = D // P
KE = E // P
QUADS = I // (4 * P)
UNITS = N * KE
STEP = 2 * QUADS
PAIRS = 4
EPS = 1e-05
C_NORM = 0
C_CW = C_NORM + KD
C_CB = C_CW + KE * DC
C_BD = C_CB + KE
C_AL = C_BD + KE
C_WD = C_AL + KE * N
SMALL = C_WD + KE

BANK_DT, BANK_BC = 0, 1
BANK_OUT = [(t + 2) % 4 for t in range(KD)]
BANK_DL = [(e + 2) % 4 for e in range(KE)]
START_JOBS = 2 + KE

NORM_F = 3 * STEP
FINISH_F = 4 * STEP
NORM_M = 5 * STEP
LOAD_H = 6 * STEP + 2
PROJECT = 5 * STEP + 6


class Walk:

    def __init__(self):
        self.n = {}
        self.reg = None
        self.start = None
        self.per = {}

    def count(self, name):
        return self.n.get(name, 0)

    def add(self, name, k=1):
        self.n[name] = self.count(name) + k

    def enter(self, reg, per):
        self.reg, self.per, self.start = reg, per, dict(self.n)

    def leave(self, reps):
        for name, v in self.n.items():
            d = v - self.start.get(name, 0)
            assert d == self.per.get(name, d), (name, d)
            self.n[name] = v + (reps - 1) * d
        self.reg = None

    def at(self, name, value=None):
        value = self.count(name) if value is None else value
        if self.reg is None or not self.per.get(name):
            return max(value, 0)
        return self.reg * self.per[name] + value


class Body:

    def __init__(self, b, ffn1, ffn2, scan, project, norm_next, reg=None, steps=8):
        self.b, self.reg = b, reg
        self.kinds = ([("G" if ffn1 else None)] * 4 + [("F" if ffn2 else None)] * 4)[8 - steps:]
        self.scan, self.project, self.norm_next = scan, project, norm_next
        self.ticks = steps * STEP
        self.ffn_pairs = 4 * sum(k is not None for k in self.kinds)
        self.first_step = next((s for s, k in enumerate(self.kinds) if k), None)
        self.side = []
        self.at_tick = []
        for tick in range(self.ticks):
            s, q = divmod(tick, STEP)
            new = []
            if ffn2 and steps == 8 and tick in (NORM_F, NORM_F + 2):
                new.append(("mean" if tick == NORM_F else "var", "F"))
            if project and tick in (NORM_M, NORM_M + 2):
                new.append(("mean" if tick == NORM_M else "var", "M"))
            if q >= 4 and s > 0 and self.kinds[s - 1]:
                new.append(("down", s - 1, q - 4))
            if project and 0 <= tick - PROJECT < 2 * KE:
                e, skip = divmod(tick - PROJECT, 2)
                new.append(("skip" if skip else "in", e))
            self.at_tick.append(new)
            self.side += new
        self.ticks_side = len(self.side)
        if norm_next:
            self.side += [("mean", "G"), ("var", "G")]
        if self.kinds[-1]:
            self.side += [("down", steps - 1, t) for t in range(KD)]

    def index(self, key):
        return self.side.index(key)

    def row(self, offset):
        return self.b + offset if self.reg is None else self.reg + (self.b + offset)


def per_body():
    full = Body(1, True, True, True, True, True)
    per = {"product_ready": 2 * full.ffn_pairs + KD + START_JOBS, "side_ready": len(full.side)}
    banks = [BANK_DT, BANK_BC] + BANK_OUT + BANK_DL
    for k in range(4):
        per[f"bank_read_{k}"] = full.ffn_pairs // 2 + banks.count(k)
    for k in range(2):
        per[f"side_read_{k}"] = len(full.side) // 2
    per.update({"magnitude_ready": 32, "hidden_ready": 8, "squares_ready": 6, "squares_read": 3, "variance_ready": 4,
                "root_ready": 4, "normed_ready": 3, "dve_step": 2 + 2 + 8 * 3 + KE * (DC - 1) + 2, "log_step": 4})
    for name in ("decay_ready", "input_ready", "state_ready", "weighted_ready", "sum_ready"):
        per[name] = UNITS
    for name in ("conv_ready", "u_ready", "gated_ready"):
        per[name] = KE
    per.update({"log_ready": 2, "delta_ready": 2, "first_term_ready": 2})
    for k in range(PAIRS):
        per[f"pair_loaded_{k}"] = 16 * full.ffn_pairs // PAIRS
    for t in range(KD):
        per[f"down_loaded_{t}"] = 16 * 8
    for k in range(2):
        per[f"mam_loaded_{k}"] = 16 * (KE + KD) // 2
        per[f"bc_loaded_{k}"] = 32 * N // 2
        per[f"u_stored_{k}"] = per[f"skip_stored_{k}"] = 16 * KE // 2
    per.update({"bc_stored": 16, "x_loaded": 16, "x1_loaded": 16, "x1_stored": 16, "res_f_free": 16,
                "u_loaded": 16, "skip_loaded": 16})
    return per


def build(nc, x_in, ffn_w, down_w, mam_w, out_w, wdt_in, wbc_in, wd2_in, small_in, out):
    f32, bf16 = mybir.dt.float32, mybir.dt.bfloat16
    ALU, ACT = mybir.AluOpType, mybir.ActivationFunctionType
    ctx = ExitStack()
    PER = per_body()

    with ctx:
        def sb(name, shape, dt=f32):
            return ctx.enter_context(nc.sbuf_tensor(name, shape, dt))

        def pb(name):
            return ctx.enter_context(nc.psum_tensor(name, [P, L], f32))

        bc_dram = nc.dram_tensor("bc_dram", [2 * N, L], f32).ap()
        x1_dram = nc.dram_tensor("x1_dram", [B, P, KD, L], f32).ap()
        skip_dram = nc.dram_tensor("skip_dram", [B, P, KE, L], f32).ap()
        u_dram = nc.dram_tensor("u_dram", [P, KE, L], f32).ap()

        wpair = [sb(f"wpair{k}", [P, 2, KD, P]) for k in range(PAIRS)]
        wdown = [sb(f"wdown{t}", [P, 4, P]) for t in range(KD)]
        wmam = [sb(f"wmam{k}", [P, KE, P]) for k in range(2)]
        wdt = sb("wdt", [P, KE, DT])
        wbc = sb("wbc", [P, KE, 2 * N])
        wd2 = sb("wd2", [P, E])
        small = sb("small", [P, SMALL])
        aneg = sb("aneg", [P, KE, N])
        ones = sb("ones", [P, P])
        G, H, F = (sb(name, [P, KD, L]) for name in ("res_g", "res_h", "res_f"))
        z = sb("z", [P, KD, L])
        zm = sb("zm", [P, KD, L])
        sq = sb("sq", [P, 2, L])
        rt, rs = sq[:, 0, :], sq[:, 1, :]
        h = [sb(f"h{k}", [P, 4, L]) for k in range(2)]
        ab = sb("ab", [P, 4, L])
        cmp = sb("cmp", [P, 6, L], bf16)
        wins = sb("wins", [P, 4, L], bf16)
        sg = [sb(f"sg{k}", [P, L]) for k in range(2)]
        y = sb("y", [P, KE, L])
        delta = sb("delta", [P, KE, L])
        du = sb("du", [P, KE, L])
        Bb = [sb(f"Bb{k}", [P, L]) for k in range(2)]
        Cb = [sb(f"Cb{k}", [P, L]) for k in range(2)]
        db = [sb(f"db{k}", [P, L]) for k in range(2)]
        hs = [sb(f"hs{k}", [P, L]) for k in range(2)]
        pr = [sb(f"pr{k}", [P, L]) for k in range(2)]
        up = [sb(f"up{k}", [P, DC - 1 + L]) for k in range(2)]
        cv = [sb(f"cv{k}", [P, L]) for k in range(2)]
        skb = [sb(f"skb{k}", [P, L]) for k in range(2)]
        bcs = pr[0][0:2 * N, :]
        dts = hs[0]
        soft = h[0]

        main = [pb(f"main{k}") for k in range(4)]
        side = [pb(f"side{k}") for k in range(2)]
        decay = [pb(f"decay{k}") for k in range(2)]

        sem = {name: ctx.enter_context(nc.semaphore(name)) for name in ["params_loaded", "const_ready", "aneg_ready", *PER]}
        PARAMS = 4

        block = ctx.enter_context(nc.Block())

        def row_of(dram, body, offset):
            return dram[bass.ds(body.row(offset), 1)].rearrange("o p k t -> (o p) k t")

        def batches(eng, walk, run, prologue, epilogue):
            prologue()
            run(Body(-1, True, False, False, True, True))
            run(Body(0, True, False, True, True, True))
            with eng.Fori(0, B - 3) as i:
                walk.enter(i, PER)
                run(Body(1, True, True, True, True, True, reg=i))
                walk.leave(B - 3)
            run(Body(B - 2, True, True, True, True, False))
            run(Body(B - 1, False, True, True, False, False))
            epilogue()
            run(Body(B, False, True, False, False, False, steps=4))

        @block.sync
        def _(sp):
            w = Walk()

            def load_pair(p):
                s, j = divmod(p, 4)
                sp.dma_start(wpair[p % PAIRS][:], ffn_w[s % 4, j]).then_inc(sem[f"pair_loaded_{p % PAIRS}"], 16)
                w.add(f"pair_loaded_{p % PAIRS}", 16)

            def load_mam(k, src):
                sp.dma_start(wmam[k][:], src).then_inc(sem[f"mam_loaded_{k}"], 16)

            def run(body):
                g0, s0, u0 = w.count("product_ready"), w.count("side_ready"), w.count("weighted_ready")
                n0, c0 = w.count("normed_ready"), w.count("u_ready")
                uses = {k: w.count(f"side_read_{k}") for k in range(2)}
                b1 = w.count("bank_read_1")

                def spread(n):
                    if n < 2:
                        sp.wait_ge(sem["bc_stored"], w.at("bc_stored"))
                    else:
                        sp.wait_ge(sem["weighted_ready"], w.at("weighted_ready", u0 + KE * (n - 1)))
                    for dst, row in ((Bb[n % 2], n), (Cb[n % 2], N + n)):
                        sp.dma_start(dst[:], bc_dram[row:row + 1, :].broadcast_to([P, L])).then_inc(sem[f"bc_loaded_{n % 2}"], 16)

                def load_down(s, t):
                    if body.kinds[s]:
                        if s and body.kinds[s - 1]:
                            sp.wait_ge(sem["side_ready"], w.at("side_ready", s0 + body.index(("down", s - 1, t)) + 1))
                        else:
                            sp.wait_ge(sem["side_ready"], w.at("side_ready", s0))
                        sp.dma_start(wdown[t][:], down_w[s % 4, t]).then_inc(sem[f"down_loaded_{t}"], 16)

                if body.scan:
                    spread(0)
                    spread(1)
                for tick in range(body.ticks):
                    s, q = divmod(tick, STEP)
                    if body.kinds[s] and q % 2 == 0:
                        p = 4 * (s - body.first_step) + q // 2 + PAIRS - 1
                        if p < body.ffn_pairs:
                            if p < PAIRS:
                                sp.wait_ge(sem["product_ready"], w.at("product_ready", g0))
                            else:
                                sp.wait_ge(sem["product_ready"], w.at("product_ready", g0 + 2 * (p - PAIRS) + 2))
                            load_pair(p)
                    if q >= 5:
                        load_down(s, q - 5)
                    if q == 0 and s:
                        load_down(s - 1, KD - 1)
                    if body.scan and tick % 4 == 1 and 2 <= (tick + 3) // 4 < N:
                        spread((tick + 3) // 4)
                    if body.project:
                        e, odd = divmod(tick - PROJECT + 2, 2)
                        if not odd and 0 <= e < KE:
                            if e < 2:
                                sp.wait_ge(sem["product_ready"], w.at("product_ready", g0))
                            else:
                                sp.wait_ge(sem["side_ready"], w.at("side_ready", s0 + body.index(("skip", e - 2)) + 1))
                            load_mam(e % 2, mam_w[e])
                        if tick == NORM_M + 2:
                            sp.wait_ge(sem["side_ready"], w.at("side_ready", s0 + body.index(("mean", "M")) + 1))
                            sp.dma_start(row_of(x1_dram, body, 1), G[:]).then_inc(sem["x1_stored"], 16)
                            w.add("x1_stored", 16)
                        if tick == PROJECT + 2 and body.norm_next:
                            sp.wait_ge(sem["x1_stored"], w.at("x1_stored"))
                            sp.wait_ge(sem["normed_ready"], w.at("normed_ready", n0 + (body.kinds[-1] is not None) + 1))
                            sp.dma_start(G[:], row_of(x_in, body, 2)).then_inc(sem["x_loaded"], 16)
                            w.add("x_loaded", 16)
                        store_tiles(body, tick, s0, c0, uses)
                load_down(len(body.kinds) - 1, KD - 1)
                w.add("product_ready", 2 * body.ffn_pairs)
                w.add("weighted_ready", UNITS if body.scan else 0)
                if body.project:
                    for tick in range(body.ticks, PROJECT + 2 * KE + 6):
                        store_tiles(body, tick, s0, c0, uses)
                    w.add("u_ready", KE)
                tail(body, s0, u0, b1, uses)

            def store_tiles(body, tick, s0, c0, uses):
                e, odd = divmod(tick - PROJECT - 3, 2)
                if not odd and 0 <= e < KE:
                    k = body.index(("skip", e))
                    sp.wait_ge(sem[f"side_read_{k % 2}"], w.at(f"side_read_{k % 2}", uses[k % 2] + k // 2 + 1))
                    sp.dma_start(row_of(skip_dram, body, 1)[:, e, :], skb[e % 2][:]).then_inc(sem[f"skip_stored_{e % 2}"], 16)
                    w.add(f"skip_stored_{e % 2}", 16)
                e, odd = divmod(tick - PROJECT - 5, 2)
                if not odd and 0 <= e < KE:
                    sp.wait_ge(sem["u_ready"], w.at("u_ready", c0 + e + 1))
                    sp.dma_start(u_dram[:, e, :], cv[e % 2][:]).then_inc(sem[f"u_stored_{e % 2}"], 16)
                    w.add(f"u_stored_{e % 2}", 16)

            def tail(body, s0, u0, b1, uses):
                if body.scan:
                    for t in range(KD):
                        if t >= 2:
                            first = w.count("product_ready") + (2 if body.project else 0)
                            sp.wait_ge(sem["product_ready"], w.at("product_ready", first + t - 1))
                        elif body.project:
                            sp.wait_ge(sem["side_ready"], w.at("side_ready", s0 + body.index(("skip", KE - 2 + t)) + 1))
                        else:
                            sp.wait_ge(sem["product_ready"], w.at("product_ready"))
                        load_mam(t % 2, out_w[t])
                if body.ffn_pairs and body.b < B:
                    sp.wait_ge(sem["product_ready"], w.at("product_ready"))
                    for p in range(PAIRS - 1):
                        load_pair(p)
                w.add("bank_read_1", body.ffn_pairs // 2)
                if body.project:
                    sp.wait_ge(sem["bank_read_1"], w.at("bank_read_1", w.count("bank_read_1") + 1))
                    sp.dma_start(bc_dram, bcs).then_inc(sem["bc_stored"], 16)
                    w.add("bc_stored", 16)
                    w.add("product_ready", START_JOBS)
                    w.add("bank_read_1", 1 + BANK_DL.count(1))
                if body.scan:
                    w.add("product_ready", KD)
                    w.add("bank_read_1")
                for k in range(2):
                    w.add(f"side_read_{k}", len(body.side) // 2)
                if body.kinds[-1] == "F":
                    for k in range(2):
                        sp.wait_ge(sem[f"side_read_{k}"], w.at(f"side_read_{k}"))
                    sp.dma_start(row_of(out, body, -1), F[:]).then_inc(sem["res_f_free"], 16)
                    w.add("res_f_free", 16)
                w.add("side_ready", len(body.side))
                w.add("normed_ready", ((body.kinds[-1] is not None) if len(body.kinds) == 8 else 0) + body.project + body.norm_next)

            def prologue():
                w.add("res_f_free", 16)
                for dst, src in ((small[:], small_in), (wdt[:], wdt_in), (wbc[:], wbc_in), (wd2[:], wd2_in)):
                    sp.dma_start(dst, src).then_inc(sem["params_loaded"], 16)
                sp.dma_start(G[:], x_in[0]).then_inc(sem["x_loaded"], 16)
                w.add("x_loaded", 16)
                for p in range(PAIRS - 1):
                    load_pair(p)
                head()

            def head():
                w.add("side_ready", 2)
                w.add("normed_ready")
                for k in range(2):
                    w.add(f"side_read_{k}")

            batches(sp, w, run, prologue, head)
            sp.wait_ge(sem["res_f_free"], w.at("res_f_free"))
            sp.wait_ge(sem["x1_stored"], w.at("x1_stored"))
            sp.wait_ge(sem["skip_stored_0"], w.at("skip_stored_0"))
            sp.wait_ge(sem["skip_stored_1"], w.at("skip_stored_1"))
            sp.wait_ge(sem["u_stored_0"], w.at("u_stored_0"))
            sp.wait_ge(sem["u_stored_1"], w.at("u_stored_1"))
            sp.wait_ge(sem["bc_stored"], w.at("bc_stored"))

        @block.tensor
        def _(pe):
            w = Walk()

            def product(bank, pairs, rows=P):
                name = f"bank_read_{bank}"
                pe.wait_ge(sem[name], w.at(name))
                w.add(name)
                for k, (lhsT, rhs) in enumerate(pairs):
                    mm = nc.tensor.matmul(main[bank][0:rows, :], lhsT, rhs, start=(k == 0), stop=(k == len(pairs) - 1))
                mm.then_inc(sem["product_ready"], 1)
                w.add("product_ready")

            def side_bank():
                k = w.count("side_ready") % 2
                pe.wait_ge(sem[f"side_read_{k}"], w.at(f"side_read_{k}"))
                w.add(f"side_read_{k}")
                w.add("side_ready")
                return side[k]

            def side_product(pairs):
                bank = side_bank()
                for k, (lhsT, rhs) in enumerate(pairs):
                    mm = nc.tensor.matmul(bank[:], lhsT, rhs, start=(k == 0), stop=(k == len(pairs) - 1))
                mm.then_inc(sem["side_ready"], 1)

            def variance():
                bank = side_bank()
                for half in range(2):
                    w.add("squares_ready")
                    pe.wait_ge(sem["squares_ready"], w.at("squares_ready"))
                    for k in range(2):
                        mm = nc.tensor.matmul(bank[:], ones[:], sq[:, k, :], start=(half + k == 0), stop=(half + k == 2))
                    if half == 0:
                        mm.then_inc(sem["squares_read"], 1)
                mm.then_inc(sem["side_ready"], 1)

            def mean(x):
                side_product([(ones[:], x[:, k, :]) for k in range(KD)])

            def weights(name):
                w.add(name, 16)
                pe.wait_ge(sem[name], w.at(name))

            def run_side(key):
                if key[0] == "mean":
                    if key[1] == "M":
                        for k in range(2):
                            pe.wait_ge(sem[f"side_read_{k}"], w.at(f"side_read_{k}"))
                    if key[1] == "F":
                        for bank in BANK_OUT:
                            pe.wait_ge(sem[f"bank_read_{bank}"], w.at(f"bank_read_{bank}", out_read[bank]))
                    mean({"M": G, "F": H, "G": G}[key[1]])
                elif key[0] == "var":
                    variance()
                elif key[0] == "down":
                    _, s, t = key
                    if t == 0:
                        w.add("hidden_ready")
                        pe.wait_ge(sem["hidden_ready"], w.at("hidden_ready"))
                    weights(f"down_loaded_{t}")
                    side_product([(wdown[t][:, j, :], h[s % 2][:, j, :]) for j in range(4)])
                else:
                    e = key[1]
                    part = 0 if key[0] == "in" else KD
                    if part == 0:
                        weights(f"mam_loaded_{e % 2}")
                        if e == 0:
                            pe.wait_ge(sem["normed_ready"], w.at("normed_ready"))
                    side_product([(wmam[e % 2][:, part + k, :], zm[:, k, :]) for k in range(KD)])

            out_read = {}

            def run(body):
                for bank in range(4):
                    out_read[bank] = w.count(f"bank_read_{bank}")
                pair = 0
                for tick in range(body.ticks):
                    s, q = divmod(tick, STEP)
                    if body.kinds[s]:
                        j, up_side = divmod(q, 2)
                        if tick == FINISH_F and len(body.kinds) == 8:
                            w.add("normed_ready")
                        if q == 0 and s % 4 == 0:
                            pe.wait_ge(sem["normed_ready"], w.at("normed_ready"))
                        if not up_side:
                            weights(f"pair_loaded_{pair % PAIRS}")
                        product(2 * (j % 2) + up_side, [(wpair[pair % PAIRS][:, up_side, k, :], z[:, k, :]) for k in range(KD)])
                        pair += up_side
                    if body.project and tick == PROJECT:
                        w.add("normed_ready")
                    for key in body.at_tick[tick]:
                        run_side(key)
                if body.project:
                    w.add("u_loaded", 16)
                    pe.wait_ge(sem["u_loaded"], w.at("u_loaded"))
                    product(BANK_DT, [(wdt[:, e, :], du[:, e, :]) for e in range(KE)])
                    product(BANK_BC, [(wbc[:, e, :], du[:, e, :]) for e in range(KE)], rows=2 * N)
                if body.norm_next:
                    w.add("x_loaded", 16)
                    pe.wait_ge(sem["x_loaded"], w.at("x_loaded"))
                    run_side(("mean", "G"))
                if body.scan:
                    w.add("gated_ready", KE)
                    pe.wait_ge(sem["gated_ready"], w.at("gated_ready"))
                    for t in range(KD):
                        weights(f"mam_loaded_{t % 2}")
                        product(BANK_OUT[t], [(wmam[t % 2][:, e, :], y[:, e, :]) for e in range(KE)])
                if body.norm_next:
                    run_side(("var", "G"))
                    w.add("normed_ready")
                if body.project:
                    pe.wait_ge(sem[f"bank_read_{BANK_DT}"], w.at(f"bank_read_{BANK_DT}", dt_read(body)))
                    for e in range(KE):
                        product(BANK_DL[e], [(wd2[:, e * P:(e + 1) * P], dts[:])])
                if body.kinds[-1]:
                    for t in range(KD):
                        run_side(("down", len(body.kinds) - 1, t))

            def dt_read(body):
                return w.count(f"bank_read_{BANK_DT}") - (BANK_OUT.count(BANK_DT) if body.scan else 0)

            def head(x):
                mean(x)
                variance()
                w.add("normed_ready")

            def prologue():
                pe.wait_ge(sem["params_loaded"], 16 * PARAMS)
                pe.wait_ge(sem["const_ready"], 1)
                w.add("x_loaded", 16)
                pe.wait_ge(sem["x_loaded"], w.at("x_loaded"))
                head(G)

            def epilogue():
                for bank in BANK_OUT:
                    pe.wait_ge(sem[f"bank_read_{bank}"], w.at(f"bank_read_{bank}"))
                head(H)

            batches(pe, w, run, prologue, epilogue)

        @block.scalar
        def _(act):
            w = Walk()

            def squares(src, mean_at, half):
                if half == 0:
                    k = mean_at % 2
                    act.wait_ge(sem["normed_ready"], w.at("normed_ready"))
                    act.wait_ge(sem[f"side_read_{k}"], w.at(f"side_read_{k}", mean_at // 2 + 1))
                else:
                    w.add("squares_read")
                    act.wait_ge(sem["squares_read"], w.at("squares_read"))
                nc.scalar.activation(sq[:], src[:, 2 * half:2 * half + 2, :], ACT.Square).then_inc(sem["squares_ready"], 1)

            def root():
                w.add("variance_ready")
                act.wait_ge(sem["variance_ready"], w.at("variance_ready"))
                nc.scalar.activation(rt, rt, ACT.Sqrt).then_inc(sem["root_ready"], 1)

            def silu(j):
                gate, up_bank = 2 * (j % 2), 2 * (j % 2) + 1
                w.add("product_ready")
                act.wait_ge(sem["product_ready"], w.at("product_ready"))
                act.wait_ge(sem[f"bank_read_{up_bank}"], w.at(f"bank_read_{up_bank}"))
                nc.scalar.activation(sg[j % 2][:], main[gate][:], ACT.Silu).then_inc(sem[f"bank_read_{gate}"], 1)
                w.add(f"bank_read_{gate}")
                w.add("product_ready")
                w.add(f"bank_read_{up_bank}")

            def magnitude(s, j):
                up_bank = 2 * (j % 2) + 1
                act.wait_ge(sem[f"bank_read_{up_bank}"], w.at(f"bank_read_{up_bank}"))
                if j == 0:
                    act.wait_ge(sem["hidden_ready"], w.at("hidden_ready"))
                nc.scalar.activation(ab[:, j, :], h[s % 2][:, j, :], ACT.Abs).then_inc(sem["magnitude_ready"], 1)
                if j == 3:
                    w.add("hidden_ready")

            def unit(u0, u):
                n, e = divmod(u, KE)
                act.wait_ge(sem["state_ready"], w.at("state_ready", u0 + u - 1))
                nc.scalar.activation(decay[u % 2][:], delta[:, e, :], ACT.Exp, scale=aneg[:, e, n:n + 1]).then_inc(sem["decay_ready"], 1)

            def run(body):
                u0, s0, c0 = w.count("state_ready"), w.count("side_ready"), w.count("conv_ready")
                k0 = w.count("skip_stored_0")
                if body.scan:
                    act.wait_ge(sem["delta_ready"], w.at("delta_ready"))

                def copy_in(e):
                    k = s0 + body.index(("in", e))
                    act.wait_ge(sem["side_ready"], w.at("side_ready", k + 1))
                    act.wait_ge(sem["conv_ready"], w.at("conv_ready", c0 + e - 1))
                    nc.scalar.activation(up[e % 2][:, DC - 1:], side[k % 2][:], ACT.Copy).then_inc(sem[f"side_read_{k % 2}"], 1)

                def silu_skip(e):
                    k = s0 + body.index(("skip", e))
                    act.wait_ge(sem["side_ready"], w.at("side_ready", k + 1))
                    act.wait_ge(sem[f"skip_stored_{e % 2}"], w.at(f"skip_stored_{e % 2}", k0 + 16 * (e // 2)))
                    nc.scalar.activation(skb[e % 2][:], side[k % 2][:], ACT.Silu).then_inc(sem[f"side_read_{k % 2}"], 1)

                def silu_u(e):
                    act.wait_ge(sem["conv_ready"], w.at("conv_ready", c0 + e + 1))
                    nc.scalar.activation(cv[e % 2][:], cv[e % 2][:], ACT.Silu).then_inc(sem["u_ready"], 1)

                def project(tick):
                    e, odd = divmod(tick - PROJECT - 1, 2)
                    if not odd and 0 <= e < KE:
                        copy_in(e)
                    e, odd = divmod(tick - PROJECT - 2, 2)
                    if not odd and 0 <= e < KE:
                        silu_skip(e)
                    e, odd = divmod(tick - PROJECT - 4, 2)
                    if not odd and 0 <= e < KE:
                        silu_u(e)

                for tick in range(body.ticks + 1):
                    s, q = divmod(tick, STEP)
                    done = (s, q // 2 - 1) if q else (s - 1, 3)
                    done = done if q % 2 == 0 and tick and body.kinds[done[0]] else None
                    if done:
                        silu(done[1])
                    if body.project:
                        project(tick)
                    for first, which, src in ((NORM_F, "F", zm), (NORM_M, "M", zm)):
                        if ("mean", which) in body.side:
                            if tick == first + 1:
                                squares(src, s0 + body.index(("mean", which)), 0)
                            if tick == first + 2:
                                squares(src, s0 + body.index(("mean", which)), 1)
                            if tick == first + 3 or (which == "M" and tick == first + 4):
                                root()
                            if tick == (FINISH_F if which == "F" else PROJECT):
                                w.add("normed_ready")
                    if body.scan and tick < body.ticks:
                        for u in range(2 * tick, 2 * tick + 2):
                            unit(u0, u)
                    if done:
                        magnitude(*done)
                    if body.scan and tick == LOAD_H:
                        if body.kinds[-1]:
                            k = s0 + body.index(("down", 4, KD - 1))
                            act.wait_ge(sem["side_read_0"], w.at("side_read_0", (k + 2) // 2))
                            act.wait_ge(sem["side_read_1"], w.at("side_read_1", (k + 1) // 2))
                        act.wait_ge(sem["x1_stored"], w.at("x1_stored"))
                        act.dma_start(H[:], row_of(x1_dram, body, 0)).then_inc(sem["x1_loaded"], 16)
                    if body.project and tick == NORM_M + 2:
                        w.add("x1_stored", 16)
                if body.project:
                    for k in range(2):
                        w.add(f"skip_stored_{k}", 16 * KE // 2)
                if body.scan:
                    for name in ("state_ready", "input_ready", "weighted_ready", "sum_ready"):
                        w.add(name, UNITS)
                    act.wait_ge(sem["weighted_ready"], w.at("weighted_ready"))
                    act.wait_ge(sem["skip_stored_0"], w.at("skip_stored_0", k0))
                    act.wait_ge(sem["skip_stored_1"], w.at("skip_stored_1", k0))
                    act.dma_start(delta[:], row_of(skip_dram, body, 0)).then_inc(sem["skip_loaded"], 16)
                if body.project:
                    for tick in range(body.ticks + 1, PROJECT + 2 * KE + 4):
                        project(tick)
                    w.add("conv_ready", KE)
                    act.wait_ge(sem["input_ready"], w.at("input_ready"))
                    for k in range(2):
                        w.add(f"u_stored_{k}", 16 * KE // 2)
                        act.wait_ge(sem[f"u_stored_{k}"], w.at(f"u_stored_{k}"))
                    act.dma_start(du[:], u_dram).then_inc(sem["u_loaded"], 16)
                    w.add("product_ready")
                    act.wait_ge(sem["product_ready"], w.at("product_ready"))
                    nc.scalar.activation(dts[:], main[BANK_DT][:], ACT.Copy).then_inc(sem[f"bank_read_{BANK_DT}"], 1)
                    w.add(f"bank_read_{BANK_DT}")
                    w.add("product_ready")
                    act.wait_ge(sem["product_ready"], w.at("product_ready"))
                    act.wait_ge(sem["sum_ready"], w.at("sum_ready"))
                    act.wait_ge(sem["bc_stored"], w.at("bc_stored"))
                    nc.scalar.activation(bcs, main[BANK_BC][0:2 * N, :], ACT.Copy).then_inc(sem[f"bank_read_{BANK_BC}"], 1)
                    w.add(f"bank_read_{BANK_BC}")
                    w.add("bc_stored", 16)
                if body.norm_next:
                    mean_at = s0 + body.index(("mean", "G"))
                    squares(z, mean_at, 0)
                    squares(z, mean_at, 1)
                if body.scan:
                    w.add("product_ready", KD)
                    for bank in BANK_OUT:
                        w.add(f"bank_read_{bank}")
                if body.norm_next:
                    root()
                    w.add("normed_ready")
                if body.project:
                    softplus()
                w.add("side_ready", len(body.side))
                for k in range(2):
                    w.add(f"side_read_{k}", len(body.side) // 2)

            def softplus():
                if w.count("log_ready"):
                    act.wait_ge(sem["delta_ready"], w.at("delta_ready"))
                act.wait_ge(sem["side_ready"], w.at("side_ready", w.count("side_ready")))
                for half in range(2):
                    es = slice(half * KE // 2, (half + 1) * KE // 2)
                    for e in range(es.start, es.stop):
                        w.add("product_ready")
                        act.wait_ge(sem["product_ready"], w.at("product_ready"))
                        nc.scalar.activation(delta[:, e, :], main[BANK_DL[e]][:], ACT.Identity,
                                             bias=small[:, C_BD + e:C_BD + e + 1]).then_inc(sem[f"bank_read_{BANK_DL[e]}"], 1)
                        w.add(f"bank_read_{BANK_DL[e]}")
                    for e in range(es.start, es.stop):
                        act.wait_ge(sem[f"bank_read_{BANK_DL[e]}"], w.at(f"bank_read_{BANK_DL[e]}"))
                    if half:
                        act.wait_ge(sem["delta_ready"], w.at("delta_ready"))
                    nc.scalar.activation(soft[:], delta[:, es, :], ACT.Abs).then_inc(sem["log_step"], 1)
                    w.add("log_step")
                    act.wait_ge(sem["log_step"], w.at("log_step"))
                    nc.scalar.activation(soft[:], soft[:], ACT.Exp, scale=-1.0).then_inc(sem["log_step"], 1)
                    w.add("log_step")
                    act.wait_ge(sem["log_step"], w.at("log_step"))
                    nc.scalar.activation(soft[:], soft[:], ACT.Ln, bias=1.0).then_inc(sem["log_ready"], 1)
                    w.add("log_ready")
                    w.add("delta_ready")

            def head(x):
                mean_at = w.count("side_ready")
                squares(x, mean_at, 0)
                squares(x, mean_at, 1)
                root()
                w.add("side_ready", 2)
                w.add("normed_ready")
                for k in range(2):
                    w.add(f"side_read_{k}")

            def prologue():
                act.wait_ge(sem["params_loaded"], 16 * PARAMS)
                nc.scalar.activation(aneg[:], small[:, C_AL:C_AL + KE * N].rearrange("p (e n) -> p e n", n=N),
                                     ACT.Exp).then_inc(sem["aneg_ready"], 1)
                act.wait_ge(sem["aneg_ready"], 1)
                nc.scalar.mul(aneg[:], aneg[:], -1.0).then_inc(sem["aneg_ready"], 1)
                act.wait_ge(sem["aneg_ready"], 2)
                head(z)

            def epilogue():
                head(zm)

            batches(act, w, run, prologue, epilogue)

        @block.vector
        def _(dve):
            w = Walk()

            def own(ins):
                ins.then_inc(sem["dve_step"], 1)
                w.add("dve_step")
                dve.wait_ge(sem["dve_step"], w.at("dve_step"))

            def centre(k, at, x, dst):
                dve.wait_ge(sem["side_ready"], w.at("side_ready", at + 1))
                nc.vector.tensor_tensor(dst[:], x[:], side[k][:].unsqueeze(1).broadcast_to([P, KD, L]),
                                        ALU.subtract).then_inc(sem[f"side_read_{k}"], 1)

            def add_eps(k, at):
                dve.wait_ge(sem["side_ready"], w.at("side_ready", at + 1))
                nc.vector.tensor_scalar(rt, side[k][:], EPS, None, ALU.add).then_inc(sem["variance_ready"], 1)

            def inverse(k):
                w.add("root_ready")
                dve.wait_ge(sem["root_ready"], w.at("root_ready"))
                nc.vector.reciprocal(rs, rt).then_inc(sem[f"side_read_{k}"], 1)

            def finish(k, at, xc):
                dve.wait_ge(sem[f"side_read_{k}"], w.at(f"side_read_{k}", at // 2 + 1))
                nc.vector.tensor_tensor(z[:], xc[:], rs.unsqueeze(1).broadcast_to([P, KD, L]),
                                        ALU.mult).then_inc(sem["normed_ready"], 1)
                w.add("normed_ready")

            def rms(k, at):
                w.add("root_ready")
                dve.wait_ge(sem["root_ready"], w.at("root_ready"))
                own(nc.vector.reciprocal(rs, rt))
                own(nc.vector.tensor_tensor(rt, rs, rs, ALU.mult))
                nc.vector.tensor_tensor(rt, rt, side[k][:], ALU.mult).then_inc(sem[f"side_read_{k}"], 1)
                dve.wait_ge(sem[f"side_read_{k}"], w.at(f"side_read_{k}", at // 2 + 1))
                nc.vector.tensor_scalar(rt, rt, EPS, None, ALU.add).then_inc(sem["variance_ready"], 1)

            def finish_mamba():
                w.add("root_ready")
                dve.wait_ge(sem["root_ready"], w.at("root_ready"))
                own(nc.vector.reciprocal(rt, rt))
                own(nc.vector.tensor_tensor(rs, rs, rt, ALU.mult))
                for k in range(KD):
                    last = nc.vector.scalar_tensor_tensor(zm[:, k, :], zm[:, k, :], small[:, C_NORM + k:C_NORM + k + 1],
                                                          rs, ALU.mult, ALU.mult)
                last.then_inc(sem["normed_ready"], 1)
                w.add("normed_ready")

            def pair(s, j):
                gate, up_bank = 2 * (j % 2), 2 * (j % 2) + 1
                w.add("product_ready", 2)
                w.add(f"bank_read_{gate}")
                dve.wait_ge(sem["product_ready"], w.at("product_ready"))
                dve.wait_ge(sem[f"bank_read_{gate}"], w.at(f"bank_read_{gate}"))
                nc.vector.tensor_tensor(h[s % 2][:, j, :], main[up_bank][:], sg[j % 2][:],
                                        ALU.mult).then_inc(sem[f"bank_read_{up_bank}"], 1)
                w.add(f"bank_read_{up_bank}")

            def compare():
                w.add("magnitude_ready", 4)
                dve.wait_ge(sem["magnitude_ready"], w.at("magnitude_ready"))
                dve.wait_ge(sem["hidden_ready"], w.at("hidden_ready"))
                for i, first in ((0, 0), (1, 3), (2, 5)):
                    m = 3 - i
                    last = nc.vector.tensor_tensor(cmp[:, first:first + m, :],
                                                   ab[:, i:i + 1, :].broadcast_to([P, m, L]), ab[:, i + 1:4, :], ALU.is_ge)
                own(last)
                nc.vector.tensor_tensor(wins[:, 0:2, :], cmp[:, 1:4:2, :], cmp[:, 2:5:2, :], ALU.add)
                own(nc.vector.tensor_tensor(wins[:, 2:4, :], cmp[:, 1:3, :], cmp[:, 3:5, :], ALU.add))

            def select(s):
                nc.vector.tensor_tensor(wins[:, 0, :], wins[:, 0, :], cmp[:, 0, :], ALU.add)
                nc.vector.tensor_tensor(wins[:, 1, :], wins[:, 1, :], cmp[:, 0, :], ALU.subtract)
                nc.vector.tensor_tensor(wins[:, 2, :], cmp[:, 5, :], wins[:, 2, :], ALU.subtract)
                own(nc.vector.tensor_tensor(wins[:, 3, :], cmp[:, 5, :], wins[:, 3, :], ALU.add))
                for i, (op, least) in enumerate(((ALU.is_ge, 2.0), (ALU.is_ge, 1.0), (ALU.is_ge, 0.0), (ALU.is_le, 1.0))):
                    last = nc.vector.scalar_tensor_tensor(h[s % 2][:, i, :], wins[:, i, :], least, h[s % 2][:, i, :], op, ALU.mult)
                last.then_inc(sem["hidden_ready"], 1)
                w.add("hidden_ready")

            def add_down(body, s0, s, t):
                k = s0 + body.index(("down", s, t))
                src, dst = (G, G) if body.kinds[s] == "G" else (H if s % 4 == 0 else F, F)
                if s == 4 or (len(body.kinds) == 4 and s == 0):
                    dve.wait_ge(sem["res_f_free"], w.at("res_f_free"))
                if s % 4:
                    before = s0 + body.index(("down", s - 1, t))
                    dve.wait_ge(sem[f"side_read_{before % 2}"], w.at(f"side_read_{before % 2}", before // 2 + 1))
                dve.wait_ge(sem["side_ready"], w.at("side_ready", k + 1))
                nc.vector.scalar_tensor_tensor(dst[:, t, :], side[k % 2][:], 0.5, src[:, t, :],
                                               ALU.mult, ALU.add).then_inc(sem[f"side_read_{k % 2}"], 1)

            def convolve(body, s0, e, c0, v0):
                k = s0 + body.index(("in", e))
                dve.wait_ge(sem[f"side_read_{k % 2}"], w.at(f"side_read_{k % 2}", k // 2 + 1))
                dve.wait_ge(sem[f"u_stored_{e % 2}"], w.at(f"u_stored_{e % 2}", v0 + 16 * (e // 2)))
                c, x = cv[e % 2], up[e % 2]
                tap = lambda k: small[:, C_CW + e * DC + k:C_CW + e * DC + k + 1]
                own(nc.vector.tensor_scalar(c[:], x[:, 0:L], tap(0), small[:, C_CB + e:C_CB + e + 1], ALU.mult, ALU.add))
                for k in range(1, DC):
                    ins = nc.vector.scalar_tensor_tensor(c[:], x[:, k:k + L], tap(k), c[:], ALU.mult, ALU.add)
                    if k < DC - 1:
                        own(ins)
                ins.then_inc(sem["conv_ready"], 1)

            def scan(u0, u):
                dve.wait_ge(sem["decay_ready"], w.at("decay_ready", u0 + u + 1))
                dve.wait_ge(sem["input_ready"], w.at("input_ready", u0 + u + 1))
                dve.wait_ge(sem["weighted_ready"], w.at("weighted_ready", u0 + u - 1))
                nc.vector.tensor_tensor_scan(hs[u % 2][:], decay[u % 2][:], db[u % 2][:], 0.0, ALU.mult,
                                             ALU.add).then_inc(sem["state_ready"], 1)

            def times_c(u0, u):
                n, e = divmod(u, KE)
                if e == 0:
                    w.add(f"bc_loaded_{n % 2}", 32)
                    dve.wait_ge(sem[f"bc_loaded_{n % 2}"], w.at(f"bc_loaded_{n % 2}"))
                dve.wait_ge(sem["state_ready"], w.at("state_ready", u0 + u + 1))
                dve.wait_ge(sem["sum_ready"], w.at("sum_ready", u0 + u - 1))
                nc.vector.tensor_tensor(pr[u % 2][:], hs[u % 2][:], Cb[n % 2][:], ALU.mult).then_inc(sem["weighted_ready"], 1)

            def run(body):
                u0, s0, c0, v0 = (w.count(n) for n in ("state_ready", "side_ready", "conv_ready", "u_stored_0"))
                norms = {}
                for which in "FMG":
                    if ("mean", which) in body.side:
                        norms[which] = s0 + body.index(("mean", which)), s0 + body.index(("var", which))
                for tick in range(body.ticks + 1):
                    s, q = divmod(tick, STEP)
                    if tick:
                        for key in body.at_tick[tick - 1]:
                            if key[0] == "down":
                                add_down(body, s0, key[1], key[2])
                    if tick == body.ticks:
                        break
                    done = (s, q // 2 - 1) if q else (s - 1, 3)
                    if q % 2 == 0 and tick and body.kinds[done[0]]:
                        pair(*done)
                    if "F" in norms:
                        mean_at, var_at = norms["F"]
                        if tick == NORM_F + 1:
                            centre(mean_at % 2, mean_at, H, zm)
                        if tick == NORM_F + 3:
                            add_eps(var_at % 2, var_at)
                        if tick == NORM_F + 4:
                            inverse(var_at % 2)
                        if tick == FINISH_F:
                            dve.wait_ge(sem["product_ready"], w.at("product_ready"))
                            finish(var_at % 2, var_at, zm)
                    if "M" in norms:
                        mean_at, var_at = norms["M"]
                        if tick == NORM_M + 1:
                            centre(mean_at % 2, mean_at, G, zm)
                        if tick == NORM_M + 3:
                            add_eps(var_at % 2, var_at)
                        if tick == NORM_M + 4:
                            rms(var_at % 2, var_at)
                        if tick == NORM_M + 5:
                            finish_mamba()
                    if body.project:
                        e, odd = divmod(tick - PROJECT - 2, 2)
                        if not odd and 0 <= e < KE:
                            convolve(body, s0, e, c0, v0)
                    if body.scan:
                        for u in range(2 * tick, 2 * tick + 2):
                            scan(u0, u)
                            if u:
                                times_c(u0, u - 1)
                    if s and body.kinds[s - 1]:
                        if q == 1:
                            compare()
                        if q == 2:
                            select(s - 1)
                if body.scan:
                    times_c(u0, UNITS - 1)
                    for name in ("state_ready", "decay_ready", "input_ready", "weighted_ready", "sum_ready"):
                        w.add(name, UNITS)
                tail(body, s0, c0, v0, norms)

            def tail(body, s0, c0, v0, norms):
                s = len(body.kinds) - 1
                if body.kinds[s]:
                    pair(s, 3)
                if body.scan:
                    dve.wait_ge(sem["sum_ready"], w.at("sum_ready"))
                    w.add("skip_loaded", 16)
                    dve.wait_ge(sem["skip_loaded"], w.at("skip_loaded"))
                    for e in range(KE):
                        nc.vector.tensor_tensor(y[:, e, :], y[:, e, :], delta[:, e, :], ALU.mult).then_inc(sem["gated_ready"], 1)
                    w.add("gated_ready", KE)
                if body.project:
                    for tick in range(body.ticks, PROJECT + 2 * KE + 2):
                        e, odd = divmod(tick - PROJECT - 2, 2)
                        if not odd and 0 <= e < KE:
                            convolve(body, s0, e, c0, v0)
                    w.add("conv_ready", KE)
                    for k in range(2):
                        w.add(f"u_stored_{k}", 16 * KE // 2)
                if body.kinds[s]:
                    compare()
                    select(s)
                if body.project:
                    w.add("product_ready", 2)
                    for bank in (BANK_DT, BANK_BC):
                        w.add(f"bank_read_{bank}")
                if body.norm_next:
                    mean_at, var_at = norms["G"]
                    centre(mean_at % 2, mean_at, G, z)
                if body.scan:
                    w.add("x1_loaded", 16)
                    dve.wait_ge(sem["x1_loaded"], w.at("x1_loaded"))
                    for t in range(KD):
                        w.add("product_ready")
                        dve.wait_ge(sem["product_ready"], w.at("product_ready"))
                        bank = BANK_OUT[t]
                        nc.vector.tensor_tensor(H[:, t, :], main[bank][:], H[:, t, :], ALU.add).then_inc(sem[f"bank_read_{bank}"], 1)
                        w.add(f"bank_read_{bank}")
                if body.norm_next:
                    add_eps(var_at % 2, var_at)
                if body.project:
                    w.add("product_ready", KE)
                    for bank in BANK_DL:
                        w.add(f"bank_read_{bank}")
                    for half in range(2):
                        es = slice(half * KE // 2, (half + 1) * KE // 2)
                        w.add("log_ready")
                        dve.wait_ge(sem["log_ready"], w.at("log_ready"))
                        nc.vector.scalar_tensor_tensor(delta[:, es, :], delta[:, es, :], 0.0, soft[:],
                                                       ALU.max, ALU.add).then_inc(sem["delta_ready"], 1)
                        w.add("delta_ready")
                        for e in range(es.start, es.stop):
                            last = nc.vector.tensor_scalar(y[:, e, :], du[:, e, :], small[:, C_WD + e:C_WD + e + 1], None, ALU.mult)
                        own(last)
                        dve.wait_ge(sem["delta_ready"], w.at("delta_ready"))
                        nc.vector.tensor_tensor(du[:, es, :], delta[:, es, :], du[:, es, :], ALU.mult).then_inc(sem["first_term_ready"], 1)
                if body.norm_next:
                    inverse(var_at % 2)
                    finish(var_at % 2, var_at, z)
                if body.kinds[s]:
                    for t in range(KD):
                        add_down(body, s0, s, t)
                    if body.kinds[s] == "F":
                        w.add("res_f_free", 16)
                w.add("side_ready", len(body.side))
                for k in range(2):
                    w.add(f"side_read_{k}", len(body.side) // 2)

            def head(x, dst):
                at = w.count("side_ready")
                w.add("side_ready", 2)
                for k in range(2):
                    w.add(f"side_read_{k}")
                centre(at % 2, at, x, dst)
                add_eps((at + 1) % 2, at + 1)
                inverse((at + 1) % 2)
                finish((at + 1) % 2, at + 1, dst)

            def prologue():
                w.add("res_f_free", 16)
                dve.wait_ge(sem["params_loaded"], 16 * PARAMS)
                dve.wait_ge(sem["const_ready"], 3)
                dve.wait_ge(sem["x_loaded"], 16)
                head(G, z)

            def epilogue():
                head(H, zm)

            batches(dve, w, run, prologue, epilogue)

        @block.gpsimd
        def _(pool):
            w = Walk()

            def scan_input(u0, u):
                n, e = divmod(u, KE)
                if e == 0:
                    w.add(f"bc_loaded_{n % 2}", 32)
                    pool.wait_ge(sem[f"bc_loaded_{n % 2}"], w.at(f"bc_loaded_{n % 2}"))
                pool.wait_ge(sem["state_ready"], w.at("state_ready", u0 + u - 1))
                nc.gpsimd.tensor_tensor(db[u % 2][:], du[:, e, :], Bb[n % 2][:], ALU.mult).then_inc(sem["input_ready"], 1)

            def sum_states(u0, u):
                e = u % KE
                pool.wait_ge(sem["weighted_ready"], w.at("weighted_ready", u0 + u + 1))
                pool.wait_ge(sem["sum_ready"], w.at("sum_ready", u0 + u - KE + 1))
                nc.gpsimd.tensor_tensor(y[:, e, :], y[:, e, :], pr[u % 2][:], ALU.add).then_inc(sem["sum_ready"], 1)

            def run(body):
                if not body.scan:
                    return
                u0 = w.count("state_ready")
                w.add("first_term_ready", 2)
                pool.wait_ge(sem["first_term_ready"], w.at("first_term_ready"))
                for u in range(UNITS):
                    scan_input(u0, u)
                    if u >= 2:
                        sum_states(u0, u - 2)
                for u in range(UNITS - 2, UNITS):
                    sum_states(u0, u)
                for name in ("state_ready", "weighted_ready", "sum_ready"):
                    w.add(name, UNITS)

            def prologue():
                nc.gpsimd.memset(F[:, 0, 0:1], 0.0).then_inc(sem["res_f_free"], 16)
                nc.gpsimd.memset(ones[:], 1.0 / D).then_inc(sem["const_ready"], 1)
                for k in range(2):
                    nc.gpsimd.memset(up[k][:, 0:DC - 1], 0.0).then_inc(sem["const_ready"], 1)

            batches(pool, w, run, prologue, lambda: None)


def _tiles(v):
    return v.reshape(-1, P).T


def kernel(L0_attn_x, L0_attn_norm_w, L0_attn_W_skip, L0_attn_W_in, L0_attn_conv_w, L0_attn_conv_b, L0_attn_Wd1,
           L0_attn_Wd2, L0_attn_bd2, L0_attn_WB, L0_attn_WC, L0_attn_A_log, L0_attn_W_D, L0_attn_W_out,
           L0_ffn_w_gate, L0_ffn_w_up, L0_ffn_w_down):
    import concourse.bacc as bacc
    from concourse.bass_utils import run_bass_kernel_spmd

    a = np.asarray
    x = a(L0_attn_x).transpose(0, 2, 1).reshape(B, KD, P, L).transpose(0, 2, 1, 3)
    cols = lambda v: a(v).reshape(KD, P, QUADS, P, 4).transpose(2, 4, 1, 0, 3)
    ffn = np.stack([cols(L0_ffn_w_gate), cols(L0_ffn_w_up)], axis=3)
    down = a(L0_ffn_w_down).reshape(QUADS, P, 4, KD, P).transpose(0, 3, 1, 2, 4)
    inner = lambda v: a(v).reshape(KE, P, KD, P).transpose(0, 3, 2, 1)
    mam = np.concatenate([inner(L0_attn_W_in), inner(L0_attn_W_skip)], axis=2)
    outer = a(L0_attn_W_out).reshape(KD, P, KE, P).transpose(0, 3, 2, 1)
    over_e = lambda v: a(v).T.reshape(KE, P, -1).transpose(1, 0, 2)
    wbc = over_e(np.concatenate([a(L0_attn_WB), a(L0_attn_WC)]))
    per_e = lambda v: a(v).reshape(KE, P, -1).transpose(1, 0, 2).reshape(P, -1)
    small = np.concatenate([_tiles(a(L0_attn_norm_w)), per_e(L0_attn_conv_w), _tiles(a(L0_attn_conv_b)),
                            _tiles(a(L0_attn_bd2)), per_e(L0_attn_A_log), _tiles(a(L0_attn_W_D))], axis=1)
    arrays = {"x_in": x, "ffn_w": ffn, "down_w": down, "mam_w": mam, "out_w": outer, "wdt_in": over_e(L0_attn_Wd1), "wbc_in": wbc,
              "wd2_in": a(L0_attn_Wd2).T, "small_in": small}
    arrays = {k: np.ascontiguousarray(v) for k, v in arrays.items()}

    nc = bacc.Bacc("TRN2", target_bir_lowering=False, num_devices=1)
    args = {k: nc.dram_tensor(k + "_dram", v.shape, mybir.dt.from_np(v.dtype), kind="ExternalInput").ap()
            for k, v in arrays.items()}
    out = nc.dram_tensor("out_dram", (B, P, KD, L), mybir.dt.float32, kind="ExternalOutput").ap()
    build(nc, out=out, **args)
    r = run_bass_kernel_spmd(nc, [{k + "_dram": v for k, v in arrays.items()}], core_ids=[0])
    got = r.results[0]["out_dram"]
    return np.ascontiguousarray(got.transpose(0, 2, 1, 3).reshape(B, D, L).transpose(0, 2, 1))
```

```python
import numpy as np
import concourse.bass as bass
from concourse import mybir
from contextlib import ExitStack


B, L, D = 8, 512, 512
E, N, DT, DC = 1024, 16, 128, 4
I = 2048
P = 128
KD = D // P
KE = E // P
QUADS = I // (4 * P)
UNITS = N * KE
STEP = 2 * QUADS
RING = 3
SLOTS = 4
RAWS = 8
AHEAD = SLOTS - 1
EPS = 1e-05
C_NORM = 0
C_CW = C_NORM + KD
C_CB = C_CW + KE * DC
C_BD = C_CB + KE
C_AL = C_BD + KE
C_WD = C_AL + KE * N
SMALL = C_WD + KE

BANK_DT, BANK_BC = 0, 1
BANK_OUT = [(t + 2) % 4 for t in range(KD)]
BANK_DL = [(e + 2) % 4 for e in range(KE)]
START_JOBS = 2 + KE

CHUNKS = KE // 2

OTHER_WORK = 6

LEAD = 16
ADD_OUT, VARIANCE_G, INVERSE_G, SCALE_G, SPLIT_G = 8, 9, 10, 11, 12
ADD_LAST = (10, 11, 13, 14)
SQUARES_G, ROOT_G = 4, 10

DOWN_TICKS = (5, 6, 7, 7), (4, 5, 6, 7)

NORM_F = 3 * STEP
FINISH_F = 4 * STEP
NORM_M = 5 * STEP
LOAD_H = 6 * STEP + 2
PROJECT = 5 * STEP + 6


class Walk:

    def __init__(self):
        self.n = {}
        self.reg = None
        self.start = None
        self.per = {}

    def count(self, name):
        return self.n.get(name, 0)

    def add(self, name, k=1):
        self.n[name] = self.count(name) + k

    def enter(self, reg, per):
        self.reg, self.per, self.start = reg, per, dict(self.n)

    def leave(self, reps):
        for name, v in self.n.items():
            d = v - self.start.get(name, 0)
            assert d == self.per.get(name, d), (name, d)
            self.n[name] = v + (reps - 1) * d
        self.reg = None

    def at(self, name, value=None):
        value = self.count(name) if value is None else value
        if self.reg is None or not self.per.get(name):
            return max(value, 0)
        return self.reg * self.per[name] + value


class Body:

    def __init__(self, b, ffn1, ffn2, scan, project, norm_next, reg=None, steps=8):
        self.b, self.reg = b, reg
        self.kinds = ([("G" if ffn1 else None)] * 4 + [("F" if ffn2 else None)] * 4)[8 - steps:]
        self.scan, self.project, self.norm_next = scan, project, norm_next
        self.split = b == -1
        self.ticks = steps * STEP
        self.units = STEP * sum(k is not None for k in self.kinds)
        self.first_step = next((s for s, k in enumerate(self.kinds) if k), None)
        self.side = []
        self.at_tick = []
        for tick in range(self.ticks):
            s, q = divmod(tick, STEP)
            new = []
            if ffn2 and steps == 8 and tick in (NORM_F, NORM_F + 2):
                new.append(("mean" if tick == NORM_F else "var", "F"))
            if project and tick in (NORM_M, NORM_M + 2):
                new.append(("mean" if tick == NORM_M else "var", "M"))
            if s > 0 and self.kinds[s - 1]:
                new += [("down", s - 1, t) for t in range(KD) if DOWN_TICKS[s > 2][t] == q]
            if project and 0 <= tick - PROJECT < 2 * KE:
                e, skip = divmod(tick - PROJECT, 2)
                new.append(("skip" if skip else "in", e))
            self.at_tick.append(new)
            self.side += new
        passes = [(3 * KD if self.kinds[tick // STEP] else 2 * KD) - OTHER_WORK + 4 * KD * len(self.at_tick[tick]) for tick in range(self.ticks)]
        if ffn1 and ffn2:
            passes[FINISH_F - 1] -= 4 * KD
        self.lead = LEAD if scan else 0
        ends = [self.lead + (UNITS - LEAD) * sum(passes[:tick + 1]) // sum(passes) if scan else 0 for tick in range(self.ticks)]
        self.units_at = [range(a, b) for a, b in zip([self.lead] + ends, ends)]
        if norm_next:
            self.side += [("mean", "G"), ("var", "G")]
        if self.kinds[-1]:
            self.side += [("down", steps - 1, t) for t in range(KD)]

    def index(self, key):
        return self.side.index(key)

    def tick_of(self, u):
        return next(tick for tick, units in enumerate(self.units_at) if u in units)

    def row(self, offset):
        return self.b + offset if self.reg is None else self.reg + (self.b + offset)


def per_body():
    full = Body(1, True, True, True, True, True)
    per = {"product_ready": full.units + KD + START_JOBS, "side_ready": len(full.side)}
    banks = [BANK_DT, BANK_BC] + BANK_OUT + BANK_DL
    for k in range(4):
        per[f"bank_read_{k}"] = full.units // 4 + banks.count(k)
    for k in range(2):
        per[f"side_read_{k}"] = len(full.side) // 2
    per.update({"magnitude_ready": 32, "quad_compared": 8, "hidden_ready": 8, "squares_ready": 6, "squares_read": 3,
                "root_ready": 3, "normed_ready": 3, "dve_step": 1 + 3 + 2 * 2 + 8 * 2 + KE * (DC - 1), "log_step": 4})
    for name in ("decay_ready", "input_ready", "state_ready", "weighted_ready", "sum_ready"):
        per[name] = UNITS
    for name in ("conv_ready", "u_ready", "gated_ready"):
        per[name] = KE
    per.update({"log_ready": 2, "delta_ready": 2, "du_ready": 2, "first_term_ready": CHUNKS, "gated_used": CHUNKS - 1})
    for k in range(SLOTS):
        per[f"unit_loaded_{k}"] = 16 * full.units // SLOTS
    for t in range(KD):
        per[f"down_loaded_{t}"] = 16 * 8
    for k in range(2):
        per[f"mam_loaded_{k}"] = 16 * ((KE + CHUNKS) // 2 + (k == 0))
        per[f"bc_loaded_{k}"] = 32 * N // 2
        per[f"u_stored_{k}"] = per[f"skip_stored_{k}"] = 16 * KE // 2
    for c in range(CHUNKS):
        per[f"y_loaded_{c}"] = 16
    per.update({"bc_stored": 16, "x_loaded": 16, "x1_loaded": 16, "x1_stored": 16, "res_f_free": 16,
                "u_loaded_0": 16, "u_loaded_1": 16, "skip_loaded": 2 * 16})
    return per


def build(nc, x_in, ffn_w, down_w, mam_w, out_w, wdt_in, wbc_in, wd2_in, small_in, out):
    f32, r32, bf16 = mybir.dt.float32, mybir.dt.float32r, mybir.dt.bfloat16
    ALU, ACT = mybir.AluOpType, mybir.ActivationFunctionType
    ctx = ExitStack()
    PER = per_body()

    with ctx:
        def sb(name, shape, dt=f32):
            return ctx.enter_context(nc.sbuf_tensor(name, shape, dt))

        def pb(name):
            return ctx.enter_context(nc.psum_tensor(name, [P, L], f32))

        bc_dram = nc.dram_tensor("bc_dram", [2 * N, L], f32).ap()
        x1_dram = nc.dram_tensor("x1_dram", [B, P, KD, L], f32).ap()
        skip_dram = nc.dram_tensor("skip_dram", [B, P, KE, L], f32).ap()
        u_dram = nc.dram_tensor("u_dram", [P, KE, L], f32).ap()

        hl_dram = nc.dram_tensor("hl_dram", [QUADS, 4, 2, P, 2, KD, P], f32).ap()

        wunit = [sb(f"wunit{k}", [P, 2, KD, P], r32) for k in range(SLOTS)]
        wdown = [sb(f"wdown{t}", [P, 4, P]) for t in range(KD)]
        wmam = [sb(f"wmam{k}", [P, KE, P]) for k in range(2)]
        wbc = sb("wbc", [P, KE, 2 * N])
        wd2 = sb("wd2", [P, E])
        small = sb("small", [P, SMALL])
        aneg = sb("aneg", [P, KE, N])
        ones = sb("ones", [P, P])
        G, H, F = (sb(name, [P, KD, L]) for name in ("res_g", "res_h", "res_f"))
        zhi = sb("zhi", [P, KD, L], r32)
        zlo = sb("zlo", [P, KD, L], r32)
        zm = sb("zm", [P, KD, L])
        h = [sb(f"h{k}", [P, 4, L]) for k in range(2)]
        ab = sb("ab", [P, 4, L])
        cmp = sb("cmp", [P, 6, L], bf16)
        wins = sb("wins", [P, 4, L], bf16)
        y = sb("y", [P, KE, L])
        delta = sb("delta", [P, KE, L])
        du = sb("du", [P, KE, L])
        Bb = [sb(f"Bb{k}", [P, L]) for k in range(2)]
        Cb = [sb(f"Cb{k}", [P, L]) for k in range(2)]
        db = [sb(f"db{k}", [P, L]) for k in range(RING)]
        hs = [sb(f"hs{k}", [P, L]) for k in range(2)]
        pr = [sb(f"pr{k}", [P, L]) for k in range(RING)]
        up = [sb(f"up{k}", [P, DC - 1 + L]) for k in range(2)]
        cv = [sb(f"cv{k}", [P, L]) for k in range(2)]
        sq = sb("sq", [P, 2, L])
        rt, rs = sq[:, 0, :], sq[:, 1, :]
        skb = [sq[:, k, :] for k in range(2)]
        raw = [y[:, k, :].rearrange("p (k m) -> p k m", k=KD) for k in range(RAWS)]
        bcs = pr[0][0:2 * N, :]
        dts = hs[0]
        skip_at = [(zhi, zlo)[e // KD][:, e % KD, :].bitcast(f32) for e in range(KE)]
        soft = h[0]

        main = [pb(f"main{k}") for k in range(4)]
        side = [pb(f"side{k}") for k in range(2)]
        decay = [pb("decay0"), pb("decay1"), sb("decay2", [P, L])]

        sem = {name: ctx.enter_context(nc.semaphore(name)) for name in
               ["params_loaded", "const_ready", "aneg_ready", "high_ready", "split_ready", *PER,
                *(f"raw_loaded_{k}" for k in range(RAWS)), *(f"split_stored_{k}" for k in range(SLOTS))]}
        PARAMS = 3

        block = ctx.enter_context(nc.Block())

        def row_of(dram, body, offset):
            return dram[bass.ds(body.row(offset), 1)].rearrange("o p k t -> (o p) k t")

        def batches(eng, walk, run, prologue, epilogue):
            prologue()
            start = Body(-1, True, False, False, True, True)
            run(start, None)
            first = Body(0, True, False, True, True, True)
            run(first, start)
            second = Body(1, True, True, True, True, True)
            run(second, first)
            with eng.Fori(0, B - 4) as i:
                walk.enter(i, PER)
                run(Body(2, True, True, True, True, True, reg=i), Body(1, True, True, True, True, True, reg=i))
                walk.leave(B - 4)
            before_last = Body(B - 2, True, True, True, True, False)
            run(before_last, Body(B - 3, True, True, True, True, True))
            last = Body(B - 1, False, True, True, False, False)
            run(last, before_last)
            epilogue(last)
            run(Body(B, False, True, False, False, False, steps=4), None)

        @block.sync
        def _(sp):
            w = Walk()

            def load_unit(n):
                s, q = divmod(n, STEP)
                sp.dma_start(wunit[n % SLOTS][:].bitcast(f32), hl_dram[s % 4, q // 2, q % 2]).then_inc(sem[f"unit_loaded_{n % SLOTS}"], 16)

            def load_raw(n):
                s, q = divmod(n, STEP)
                sp.dma_start(raw[n % RAWS], ffn_w[s, q // 2, q % 2]).then_inc(sem[f"raw_loaded_{n % RAWS}"], 16)

            def store_split(n):
                s, q = divmod(n, STEP)
                sp.wait_ge(sem["split_ready"], n + 1)
                sp.dma_start(hl_dram[s, q // 2, q % 2], wunit[n % SLOTS][:].bitcast(f32)).then_inc(sem[f"split_stored_{n % SLOTS}"], 16)

            def load_bc(n):
                for dst, row in ((Bb[n % 2], n), (Cb[n % 2], N + n)):
                    sp.dma_start(dst[:], bc_dram[row:row + 1, :].broadcast_to([P, L])).then_inc(sem[f"bc_loaded_{n % 2}"], 16)

            def store_out(body):
                for k in range(2):
                    sp.wait_ge(sem[f"side_read_{k}"], w.at(f"side_read_{k}"))
                sp.dma_start(row_of(out, body, -1), F[:]).then_inc(sem["res_f_free"], 16)
                w.add("res_f_free", 16)

            def load_mam(k, src):
                sp.dma_start(wmam[k][:], src).then_inc(sem[f"mam_loaded_{k}"], 16)

            def run(body, prev):
                g0, s0, u0 = w.count("product_ready"), w.count("side_ready"), w.count("weighted_ready")
                n0, c0 = w.count("normed_ready"), w.count("u_ready")
                uses = {k: w.count(f"side_read_{k}") for k in range(2)}
                b1 = w.count("bank_read_1")

                def spread(n):
                    sp.wait_ge(sem["weighted_ready"], w.at("weighted_ready", u0 + KE * (n - 1)))
                    load_bc(n)

                def load_down(s, t):
                    if body.kinds[s]:
                        if s and body.kinds[s - 1]:
                            sp.wait_ge(sem["side_ready"], w.at("side_ready", s0 + body.index(("down", s - 1, t)) + 1))
                        else:
                            sp.wait_ge(sem["side_ready"], w.at("side_ready", s0))
                        sp.dma_start(wdown[t][:], down_w[s % 4, t]).then_inc(sem[f"down_loaded_{t}"], 16)

                for n in range(2, N if body.scan else 0):
                    if KE * (n - 1) < body.lead:
                        spread(n)
                for tick in range(body.ticks):
                    s, q = divmod(tick, STEP)
                    if tick == 1 and prev and prev.kinds[-1] == "F":
                        store_out(prev)
                    if body.split and body.kinds[s]:
                        if tick + RAWS - 2 < body.units:
                            if tick >= 2:
                                sp.wait_ge(sem["split_ready"], tick - 1)
                            load_raw(tick + RAWS - 2)
                        if tick + 2 < body.units:
                            store_split(tick + 2)
                    elif body.kinds[s]:
                        n = tick - STEP * body.first_step
                        if n + AHEAD < body.units:
                            sp.wait_ge(sem["product_ready"], w.at("product_ready", g0 + n))
                            load_unit(n + AHEAD)
                    if q >= 5:
                        load_down(s, q - 5)
                    if q == 0 and s:
                        load_down(s - 1, KD - 1)
                    for n in range(2, N if body.scan else 0):
                        if KE * (n - 1) >= body.lead and tick == body.tick_of(KE * (n - 1)) + 1:
                            spread(n)
                    if body.project:
                        e, odd = divmod(tick - PROJECT + 2, 2)
                        if not odd and 0 <= e < KE:
                            if e < 2:
                                sp.wait_ge(sem["product_ready"], w.at("product_ready", g0))
                            else:
                                sp.wait_ge(sem["side_ready"], w.at("side_ready", s0 + body.index(("skip", e - 2)) + 1))
                            load_mam(e % 2, mam_w[e])
                        if tick == NORM_M + 2:
                            sp.wait_ge(sem["side_ready"], w.at("side_ready", s0 + body.index(("mean", "M")) + 1))
                            sp.dma_start(row_of(x1_dram, body, 1), G[:]).then_inc(sem["x1_stored"], 16)
                            w.add("x1_stored", 16)
                        if tick == PROJECT + 2 and body.norm_next:
                            sp.wait_ge(sem["x1_stored"], w.at("x1_stored"))
                            sp.wait_ge(sem["normed_ready"], w.at("normed_ready", n0 + (body.kinds[-1] is not None) + 1))
                            sp.dma_start(G[:], row_of(x_in, body, 2)).then_inc(sem["x_loaded"], 16)
                            w.add("x_loaded", 16)
                        store_tiles(body, tick, s0, c0, uses)
                load_down(len(body.kinds) - 1, KD - 1)
                w.add("product_ready", body.units)
                w.add("weighted_ready", UNITS if body.scan else 0)
                if body.project:
                    for tick in range(body.ticks, PROJECT + 2 * KE + 6):
                        store_tiles(body, tick, s0, c0, uses)
                    w.add("u_ready", KE)
                tail(body, s0, u0, b1, uses)

            def store_tiles(body, tick, s0, c0, uses):
                e, odd = divmod(tick - PROJECT - 3, 2)
                if not odd and 0 <= e < KE:
                    k = body.index(("skip", e))
                    sp.wait_ge(sem[f"side_read_{k % 2}"], w.at(f"side_read_{k % 2}", uses[k % 2] + k // 2 + 1))
                    sp.dma_start(row_of(skip_dram, body, 1)[:, e, :], skb[e % 2]).then_inc(sem[f"skip_stored_{e % 2}"], 16)
                    w.add(f"skip_stored_{e % 2}", 16)
                e, odd = divmod(tick - PROJECT - 5, 2)
                if not odd and 0 <= e < KE:
                    sp.wait_ge(sem["u_ready"], w.at("u_ready", c0 + e + 1))
                    sp.dma_start(u_dram[:, e, :], cv[e % 2][:]).then_inc(sem[f"u_stored_{e % 2}"], 16)
                    w.add(f"u_stored_{e % 2}", 16)

            def tail(body, s0, u0, b1, uses):
                if body.project:
                    sp.wait_ge(sem["side_ready"], w.at("side_ready", s0 + body.index(("skip", KE - 2)) + 1))
                    load_mam(0, wdt_in)
                done = w.count("product_ready")
                if body.scan:
                    if body.project:
                        sp.wait_ge(sem["side_ready"], w.at("side_ready", s0 + body.index(("skip", KE - 1)) + 1))
                    else:
                        sp.wait_ge(sem["product_ready"], w.at("product_ready"))
                    load_mam(1, out_w[0])
                    if body.project:
                        sp.wait_ge(sem["product_ready"], w.at("product_ready", done + 1))
                    load_mam(0, out_w[1])
                if body.b < B:
                    sp.wait_ge(sem["product_ready"], w.at("product_ready"))
                    if body.split:
                        for k in range(SLOTS):
                            sp.wait_ge(sem[f"split_stored_{k}"], 16 * body.units // SLOTS)
                    for n in range(AHEAD):
                        load_unit(n)
                w.add("bank_read_1", body.units // 4)
                if body.project:
                    sp.wait_ge(sem["bank_read_1"], w.at("bank_read_1", w.count("bank_read_1") + 2))
                    sp.dma_start(bc_dram, bcs).then_inc(sem["bc_stored"], 16)
                    w.add("bc_stored", 16)
                    w.add("product_ready", START_JOBS)
                    w.add("bank_read_1", 1 + BANK_DL.count(1))
                    sp.wait_ge(sem["bc_stored"], w.at("bc_stored"))
                    load_bc(0)
                    load_bc(1)
                if body.scan:
                    w.add("product_ready", KD)
                    w.add("bank_read_1")
                used = w.count("gated_used")
                for c in range(CHUNKS):
                    if body.scan and c < CHUNKS - 1:
                        sp.wait_ge(sem["gated_used"], w.at("gated_used", used + c + 1))
                        w.add("gated_used")
                    elif body.scan:
                        sp.wait_ge(sem["product_ready"], w.at("product_ready"))
                    if body.project:
                        if c == 0:
                            for k in range(2):
                                sp.wait_ge(sem[f"u_stored_{k}"], w.at(f"u_stored_{k}"))
                            if body.split:
                                sp.wait_ge(sem["split_ready"], body.units)
                        sp.dma_start(y[:, 2 * c:2 * c + 2, :], u_dram[:, 2 * c:2 * c + 2, :]).then_inc(sem[f"y_loaded_{c}"], 16)
                    if body.scan and c + 2 < CHUNKS:
                        load_mam((c + 1) % 2, out_w[c + 2])
                for k in range(2):
                    w.add(f"side_read_{k}", len(body.side) // 2)
                w.add("side_ready", len(body.side))
                w.add("normed_ready", ((body.kinds[-1] is not None) if len(body.kinds) == 8 else 0) + body.project + body.norm_next)

            def prologue():
                w.add("res_f_free", 16)
                for dst, src in ((small[:], small_in), (wbc[:], wbc_in), (wd2[:], wd2_in)):
                    sp.dma_start(dst, src).then_inc(sem["params_loaded"], 16)
                sp.dma_start(G[:], x_in[0]).then_inc(sem["x_loaded"], 16)
                w.add("x_loaded", 16)
                for n in range(RAWS - 2):
                    load_raw(n)
                for n in range(2):
                    store_split(n)
                head()

            def head():
                w.add("side_ready", 2)
                w.add("normed_ready")
                for k in range(2):
                    w.add(f"side_read_{k}")

            def epilogue(prev):
                store_out(prev)
                head()

            batches(sp, w, run, prologue, epilogue)
            store_out(Body(B, False, True, False, False, False, steps=4))
            sp.wait_ge(sem["res_f_free"], w.at("res_f_free"))
            sp.wait_ge(sem["x1_stored"], w.at("x1_stored"))
            sp.wait_ge(sem["skip_stored_0"], w.at("skip_stored_0"))
            sp.wait_ge(sem["skip_stored_1"], w.at("skip_stored_1"))
            sp.wait_ge(sem["u_stored_0"], w.at("u_stored_0"))
            sp.wait_ge(sem["u_stored_1"], w.at("u_stored_1"))
            sp.wait_ge(sem["bc_stored"], w.at("bc_stored"))

        @block.tensor
        def _(pe):
            w = Walk()

            def product(bank, pairs, rows=P):
                name = f"bank_read_{bank}"
                pe.wait_ge(sem[name], w.at(name))
                w.add(name)
                for k, (lhsT, rhs) in enumerate(pairs):
                    mm = nc.tensor.matmul(main[bank][0:rows, :], lhsT, rhs, start=(k == 0), stop=(k == len(pairs) - 1))
                mm.then_inc(sem["product_ready"], 1)
                w.add("product_ready")

            def side_bank():
                k = w.count("side_ready") % 2
                pe.wait_ge(sem[f"side_read_{k}"], w.at(f"side_read_{k}"))
                w.add(f"side_read_{k}")
                w.add("side_ready")
                return side[k]

            def side_product(pairs):
                bank = side_bank()
                for k, (lhsT, rhs) in enumerate(pairs):
                    mm = nc.tensor.matmul(bank[:], lhsT, rhs, start=(k == 0), stop=(k == len(pairs) - 1))
                mm.then_inc(sem["side_ready"], 1)

            def variance_half(half, bank):
                w.add("squares_ready")
                pe.wait_ge(sem["squares_ready"], w.at("squares_ready"))
                for k in range(2):
                    mm = nc.tensor.matmul(bank[:], ones[:], sq[:, k, :], start=(half + k == 0), stop=(half + k == 2))
                mm.then_inc(sem["side_ready" if half else "squares_read"], 1)

            def variance():
                bank = side_bank()
                variance_half(0, bank)
                variance_half(1, bank)

            def mean(x):
                side_product([(ones[:], x[:, k, :]) for k in range(KD)])

            def weights(name):
                w.add(name, 16)
                pe.wait_ge(sem[name], w.at(name))

            def run_side(key):
                if key[0] == "mean":
                    if key[1] == "M":
                        for k in range(2):
                            pe.wait_ge(sem[f"side_read_{k}"], w.at(f"side_read_{k}"))
                    if key[1] == "F":
                        for bank in BANK_OUT:
                            pe.wait_ge(sem[f"bank_read_{bank}"], w.at(f"bank_read_{bank}", out_read[bank]))
                    mean({"M": G, "F": H, "G": G}[key[1]])
                elif key[0] == "var":
                    variance()
                elif key[0] == "down":
                    _, s, t = key
                    if t == 0:
                        w.add("hidden_ready")
                        pe.wait_ge(sem["hidden_ready"], w.at("hidden_ready"))
                    weights(f"down_loaded_{t}")
                    side_product([(wdown[t][:, j, :], h[s % 2][:, j, :]) for j in range(4)])
                else:
                    e = key[1]
                    part = 0 if key[0] == "in" else KD
                    if part == 0:
                        weights(f"mam_loaded_{e % 2}")
                        if e == 0:
                            pe.wait_ge(sem["normed_ready"], w.at("normed_ready"))
                    side_product([(wmam[e % 2][:, part + k, :], zm[:, k, :]) for k in range(KD)])

            out_read = {}

            def run(body, prev):
                for bank in range(4):
                    out_read[bank] = w.count(f"bank_read_{bank}")
                for tick in range(body.ticks):
                    s, q = divmod(tick, STEP)
                    if body.kinds[s]:
                        j, up_side = divmod(q, 2)
                        if tick == FINISH_F and len(body.kinds) == 8:
                            w.add("normed_ready")
                        if q == 0 and s % 4 == 0:
                            pe.wait_ge(sem["normed_ready"], w.at("normed_ready"))
                        if body.split:
                            pe.wait_ge(sem["split_ready"], tick + 1)
                        else:
                            weights(f"unit_loaded_{q % SLOTS}")
                        hi, lo = wunit[q % SLOTS][:, 0], wunit[q % SLOTS][:, 1]
                        product(2 * (j % 2) + up_side, [(part[:, k, :], x[:, k, :]) for k in range(KD)
                                                        for part, x in ((hi, zhi), (hi, zlo), (lo, zhi))])
                    if body.project and tick == PROJECT:
                        w.add("normed_ready")
                    for key in body.at_tick[tick]:
                        run_side(key)
                if body.norm_next:
                    w.add("x_loaded", 16)
                    pe.wait_ge(sem["x_loaded"], w.at("x_loaded"))
                    run_side(("mean", "G"))
                if body.project:
                    weights("mam_loaded_0")
                    pe.wait_ge(sem[f"bank_read_{BANK_DT}"], w.at(f"bank_read_{BANK_DT}"))
                    w.add(f"bank_read_{BANK_DT}")
                    for e in range(KE):
                        if e % (KE // 2) == 0:
                            half = 2 * e // KE
                            w.add(f"u_loaded_{half}", 16)
                            pe.wait_ge(sem[f"u_loaded_{half}"], w.at(f"u_loaded_{half}"))
                        mm = nc.tensor.matmul(main[BANK_DT][:], wmam[0][:, e, :], du[:, e, :], start=(e == 0), stop=(e == KE - 1))
                    mm.then_inc(sem["product_ready"], 1)
                    w.add("product_ready")
                    pe.wait_ge(sem[f"bank_read_{BANK_DT}"], w.at(f"bank_read_{BANK_DT}"))
                    for e in range(KE):
                        if e == KE // 2:
                            product(BANK_BC, [(wbc[:, k, :], du[:, k, :]) for k in range(KE)], rows=2 * N)
                        product(BANK_DL[e], [(wd2[:, e * P:(e + 1) * P], dts[:])])
                if body.scan:
                    w.add("gated_ready", KE)
                    pe.wait_ge(sem["gated_ready"], w.at("gated_ready"))
                    bank = side_bank() if body.norm_next else None
                    project_out(bank)
                    if body.norm_next:
                        variance_half(1, bank)
                elif body.norm_next:
                    variance()
                if body.norm_next:
                    w.add("normed_ready")
                if body.kinds[-1]:
                    for t in range(KD):
                        run_side(("down", len(body.kinds) - 1, t))

            def project_out(bank):
                for k in BANK_OUT:
                    pe.wait_ge(sem[f"bank_read_{k}"], w.at(f"bank_read_{k}"))
                    w.add(f"bank_read_{k}")
                for e in range(KE):
                    if e == KE // 2 + 1 and bank:
                        variance_half(0, bank)
                    c, odd = divmod(e, 2)
                    if not odd:
                        weights(f"mam_loaded_{(c + 1) % 2}")
                    for t in range(KD):
                        mm = nc.tensor.matmul(main[BANK_OUT[t]][:], wmam[(c + 1) % 2][:, odd * KD + t, :], y[:, e, :],
                                              start=(e == 0), stop=(e == KE - 1))
                        if e == KE - 1:
                            mm.then_inc(sem["product_ready"], 1)
                            w.add("product_ready")
                    if odd and e < KE - 1:
                        mm.then_inc(sem["gated_used"], 1)

            def head(x):
                mean(x)
                variance()
                w.add("normed_ready")

            def prologue():
                pe.wait_ge(sem["params_loaded"], 16 * PARAMS)
                pe.wait_ge(sem["const_ready"], 1)
                w.add("x_loaded", 16)
                pe.wait_ge(sem["x_loaded"], w.at("x_loaded"))
                head(G)

            def epilogue(prev):
                for bank in BANK_OUT:
                    pe.wait_ge(sem[f"bank_read_{bank}"], w.at(f"bank_read_{bank}"))
                head(H)

            batches(pe, w, run, prologue, epilogue)

        @block.scalar
        def _(act):
            w = Walk()

            def squares(src, mean_at, half):
                if half == 0:
                    k = mean_at % 2
                    act.wait_ge(sem["normed_ready"], w.at("normed_ready"))
                    act.wait_ge(sem[f"side_read_{k}"], w.at(f"side_read_{k}", mean_at // 2 + 1))
                else:
                    w.add("squares_read")
                    act.wait_ge(sem["squares_read"], w.at("squares_read"))
                nc.scalar.activation(sq[:], src[:, 2 * half:2 * half + 2, :], ACT.Square).then_inc(sem["squares_ready"], 1)

            def root(var_at):
                k = var_at % 2
                act.wait_ge(sem[f"side_read_{k}"], w.at(f"side_read_{k}", var_at // 2 + 1))
                nc.scalar.activation(rt, rt, ACT.Sqrt).then_inc(sem["root_ready"], 1)

            def silu(s, j):
                gate, up_bank = 2 * (j % 2), 2 * (j % 2) + 1
                w.add("product_ready")
                act.wait_ge(sem["product_ready"], w.at("product_ready"))
                act.wait_ge(sem[f"bank_read_{up_bank}"], w.at(f"bank_read_{up_bank}"))
                nc.scalar.activation(h[s % 2][:, j, :], main[gate][:], ACT.Silu).then_inc(sem[f"bank_read_{gate}"], 1)
                w.add(f"bank_read_{gate}")
                w.add("product_ready")
                w.add(f"bank_read_{up_bank}")

            def split_high(n):
                act.wait_ge(sem[f"raw_loaded_{n % RAWS}"], 16 * (n // RAWS + 1))
                if n >= SLOTS:
                    act.wait_ge(sem["product_ready"], n - SLOTS + 1)
                    act.wait_ge(sem[f"split_stored_{n % SLOTS}"], 16 * (n // SLOTS))
                nc.scalar.activation(wunit[n % SLOTS][:, 0], raw[n % RAWS], ACT.Copy).then_inc(sem["high_ready"], 1)

            def magnitude(s, j):
                up_bank = 2 * (j % 2) + 1
                act.wait_ge(sem[f"bank_read_{up_bank}"], w.at(f"bank_read_{up_bank}"))
                if j == 0:
                    act.wait_ge(sem["quad_compared"], w.at("quad_compared"))
                nc.scalar.activation(ab[:, j, :], h[s % 2][:, j, :], ACT.Abs).then_inc(sem["magnitude_ready"], 1)
                if j == 3:
                    w.add("quad_compared")

            def unit(u0, u):
                n, e = divmod(u, KE)
                act.wait_ge(sem["state_ready"], w.at("state_ready", u0 + u - RING + 1))
                nc.scalar.activation(decay[u % RING][:], delta[:, e, :], ACT.Exp, scale=aneg[:, e, n:n + 1]).then_inc(sem["decay_ready"], 1)

            def run(body, prev):
                u0, s0, c0 = w.count("state_ready"), w.count("side_ready"), w.count("conv_ready")
                k0, v0 = w.count("skip_stored_0"), w.count("u_stored_0")
                if body.scan:
                    act.wait_ge(sem["delta_ready"], w.at("delta_ready"))

                def copy_in(e):
                    k = s0 + body.index(("in", e))
                    act.wait_ge(sem["side_ready"], w.at("side_ready", k + 1))
                    act.wait_ge(sem["conv_ready"], w.at("conv_ready", c0 + e - 1))
                    nc.scalar.activation(up[e % 2][:, DC - 1:], side[k % 2][:], ACT.Copy).then_inc(sem[f"side_read_{k % 2}"], 1)

                def silu_skip(e):
                    k = s0 + body.index(("skip", e))
                    act.wait_ge(sem["side_ready"], w.at("side_ready", k + 1))
                    act.wait_ge(sem[f"skip_stored_{e % 2}"], w.at(f"skip_stored_{e % 2}", k0 + 16 * (e // 2)))
                    nc.scalar.activation(skb[e % 2], side[k % 2][:], ACT.Silu).then_inc(sem[f"side_read_{k % 2}"], 1)

                def silu_u(e):
                    act.wait_ge(sem["conv_ready"], w.at("conv_ready", c0 + e + 1))
                    nc.scalar.activation(cv[e % 2][:], cv[e % 2][:], ACT.Silu).then_inc(sem["u_ready"], 1)

                def load_u(half):
                    if body.scan:
                        act.wait_ge(sem["input_ready"], w.at("input_ready", u0 + UNITS - (0 if half else KE // 2)))
                    for k in range(2):
                        act.wait_ge(sem[f"u_stored_{k}"], w.at(f"u_stored_{k}", v0 + 16 * (half + 1) * KE // 4))
                    es = slice(half * KE // 2, (half + 1) * KE // 2)
                    act.dma_start(du[:, es, :], u_dram[:, es, :]).then_inc(sem[f"u_loaded_{half}"], 16)

                def load_skip():
                    act.wait_ge(sem["product_ready"], w.at("product_ready"))
                    act.wait_ge(sem["skip_stored_0"], w.at("skip_stored_0", k0))
                    act.wait_ge(sem["skip_stored_1"], w.at("skip_stored_1", k0))
                    for first, part in ((0, zhi), (KD, zlo)):
                        act.dma_start(part[:].bitcast(f32), row_of(skip_dram, body, 0)[:, first:first + KD, :]).then_inc(sem["skip_loaded"], 16)

                def project(tick):
                    e, odd = divmod(tick - PROJECT - 1, 2)
                    if not odd and 0 <= e < KE:
                        copy_in(e)
                    e, odd = divmod(tick - PROJECT - 2, 2)
                    if not odd and 0 <= e < KE:
                        silu_skip(e)
                    e, odd = divmod(tick - PROJECT - 4, 2)
                    if not odd and 0 <= e < KE:
                        silu_u(e)

                for u in range(body.lead):
                    if u == SQUARES_G and prev.norm_next:
                        squares(zm, s0 - len(prev.side) + prev.index(("mean", "G")), 1)
                    if u == ROOT_G and prev.norm_next:
                        root(s0 - len(prev.side) + prev.index(("var", "G")))
                        w.add("normed_ready")
                    unit(u0, u)
                for tick in range(body.ticks + 1):
                    s, q = divmod(tick, STEP)
                    done = (s, q // 2 - 1) if q else (s - 1, 3)
                    done = done if q % 2 == 0 and tick and body.kinds[done[0]] else None
                    units = body.units_at[tick] if tick < body.ticks else range(0)
                    for u in units[:2]:
                        unit(u0, u)
                    if done:
                        silu(*done)
                    if body.split and tick + AHEAD < body.units:
                        split_high(tick + AHEAD)
                    if body.project:
                        project(tick)
                    for first, which, src in ((NORM_F, "F", zm), (NORM_M, "M", zm)):
                        if ("mean", which) in body.side:
                            if tick == first + 1:
                                squares(src, s0 + body.index(("mean", which)), 0)
                            if tick == first + 2:
                                squares(src, s0 + body.index(("mean", which)), 1)
                            if tick == first + 3:
                                root(s0 + body.index(("var", which)))
                            if tick == (FINISH_F if which == "F" else PROJECT):
                                w.add("normed_ready")
                    for u in units[2:]:
                        unit(u0, u)
                    if tick == body.ticks:
                        if body.project:
                            load_u(0)
                            load_u(1)
                        if body.scan:
                            load_skip()
                    if done:
                        magnitude(*done)
                    if body.scan and tick == LOAD_H:
                        if body.kinds[-1]:
                            k = s0 + body.index(("down", 4, KD - 1))
                            act.wait_ge(sem["side_read_0"], w.at("side_read_0", (k + 2) // 2))
                            act.wait_ge(sem["side_read_1"], w.at("side_read_1", (k + 1) // 2))
                        act.wait_ge(sem["x1_stored"], w.at("x1_stored"))
                        act.dma_start(H[:], row_of(x1_dram, body, 0)).then_inc(sem["x1_loaded"], 16)
                    if body.project and tick == NORM_M + 2:
                        w.add("x1_stored", 16)
                if body.project:
                    for k in range(2):
                        w.add(f"skip_stored_{k}", 16 * KE // 2)
                if body.scan:
                    for name in ("state_ready", "input_ready", "weighted_ready", "sum_ready"):
                        w.add(name, UNITS)
                if body.project:
                    w.add("conv_ready", KE)
                    for k in range(2):
                        w.add(f"u_stored_{k}", 16 * KE // 2)
                if body.project:
                    w.add("product_ready")
                    act.wait_ge(sem["product_ready"], w.at("product_ready"))
                    if body.scan:
                        act.wait_ge(sem["weighted_ready"], w.at("weighted_ready"))
                    nc.scalar.activation(dts[:], main[BANK_DT][:], ACT.Copy).then_inc(sem[f"bank_read_{BANK_DT}"], 1)
                    w.add(f"bank_read_{BANK_DT}")
                if body.project:
                    softplus()
                if body.norm_next:
                    mean_at = s0 + body.index(("mean", "G"))
                    for k in range(2):
                        act.wait_ge(sem[f"skip_stored_{k}"], w.at(f"skip_stored_{k}"))
                    squares(zm, mean_at, 0)
                if body.scan:
                    w.add("product_ready", KD)
                    for bank in BANK_OUT:
                        w.add(f"bank_read_{bank}")
                w.add("side_ready", len(body.side))
                for k in range(2):
                    w.add(f"side_read_{k}", len(body.side) // 2)

            def copy_bc():
                w.add("product_ready")
                act.wait_ge(sem["product_ready"], w.at("product_ready"))
                act.wait_ge(sem["sum_ready"], w.at("sum_ready"))
                act.wait_ge(sem["bc_stored"], w.at("bc_stored"))
                nc.scalar.activation(bcs, main[BANK_BC][0:2 * N, :], ACT.Copy).then_inc(sem[f"bank_read_{BANK_BC}"], 1)
                w.add(f"bank_read_{BANK_BC}")
                w.add("bc_stored", 16)

            def softplus():
                if w.count("log_ready"):
                    act.wait_ge(sem["delta_ready"], w.at("delta_ready"))
                act.wait_ge(sem["side_ready"], w.at("side_ready", w.count("side_ready")))
                for half in range(2):
                    es = slice(half * KE // 2, (half + 1) * KE // 2)
                    for e in range(es.start, es.stop):
                        w.add("product_ready")
                        act.wait_ge(sem["product_ready"], w.at("product_ready"))
                        nc.scalar.activation(delta[:, e, :], main[BANK_DL[e]][:], ACT.Identity,
                                             bias=small[:, C_BD + e:C_BD + e + 1]).then_inc(sem[f"bank_read_{BANK_DL[e]}"], 1)
                        w.add(f"bank_read_{BANK_DL[e]}")
                    for e in range(es.start, es.stop):
                        act.wait_ge(sem[f"bank_read_{BANK_DL[e]}"], w.at(f"bank_read_{BANK_DL[e]}"))
                    if half:
                        act.wait_ge(sem["delta_ready"], w.at("delta_ready"))
                    nc.scalar.activation(soft[:], delta[:, es, :], ACT.Abs).then_inc(sem["log_step"], 1)
                    w.add("log_step")
                    act.wait_ge(sem["log_step"], w.at("log_step"))
                    nc.scalar.activation(soft[:], soft[:], ACT.Exp, scale=-1.0).then_inc(sem["log_step"], 1)
                    w.add("log_step")
                    act.wait_ge(sem["log_step"], w.at("log_step"))
                    nc.scalar.activation(soft[:], soft[:], ACT.Ln, bias=1.0).then_inc(sem["log_ready"], 1)
                    w.add("log_ready")
                    w.add("delta_ready")
                    if half == 0:
                        copy_bc()

            def head(x):
                mean_at = w.count("side_ready")
                squares(x, mean_at, 0)
                squares(x, mean_at, 1)
                root(mean_at + 1)
                w.add("side_ready", 2)
                w.add("normed_ready")
                for k in range(2):
                    w.add(f"side_read_{k}")

            def prologue():
                act.wait_ge(sem["params_loaded"], 16 * PARAMS)
                nc.scalar.activation(aneg[:], small[:, C_AL:C_AL + KE * N].rearrange("p (e n) -> p e n", n=N),
                                     ACT.Exp).then_inc(sem["aneg_ready"], 1)
                act.wait_ge(sem["aneg_ready"], 1)
                nc.scalar.mul(aneg[:], aneg[:], -1.0).then_inc(sem["aneg_ready"], 1)
                act.wait_ge(sem["aneg_ready"], 2)
                for n in range(AHEAD):
                    split_high(n)
                head(zm)

            def epilogue(prev):
                head(zm)

            batches(act, w, run, prologue, epilogue)

        @block.vector
        def _(dve):
            w = Walk()

            def own(ins):
                ins.then_inc(sem["dve_step"], 1)
                w.add("dve_step")
                dve.wait_ge(sem["dve_step"], w.at("dve_step"))

            def centre(k, at, x):
                dve.wait_ge(sem["side_ready"], w.at("side_ready", at + 1))
                nc.vector.tensor_tensor(zm[:], x[:], side[k][:].unsqueeze(1).broadcast_to([P, KD, L]),
                                        ALU.subtract).then_inc(sem[f"side_read_{k}"], 1)

            def add_eps(k, at):
                dve.wait_ge(sem["side_ready"], w.at("side_ready", at + 1))
                nc.vector.tensor_scalar(rt, side[k][:], EPS, None, ALU.add).then_inc(sem[f"side_read_{k}"], 1)

            def inverse():
                w.add("root_ready")
                dve.wait_ge(sem["root_ready"], w.at("root_ready"))
                own(nc.vector.reciprocal(rs, rt))

            def scale():
                own(nc.vector.tensor_tensor(zm[:], zm[:], rs.unsqueeze(1).broadcast_to([P, KD, L]), ALU.mult))

            def split_input():
                own(nc.vector.tensor_copy(zhi[:], zm[:]))
                nc.vector.tensor_tensor(zlo[:], zm[:], zhi[:], ALU.subtract).then_inc(sem["normed_ready"], 1)
                w.add("normed_ready")

            def split_low(n):
                dve.wait_ge(sem["high_ready"], n + 1)
                nc.vector.tensor_tensor(wunit[n % SLOTS][:, 1], raw[n % RAWS], wunit[n % SLOTS][:, 0],
                                        ALU.subtract).then_inc(sem["split_ready"], 1)

            def rms_eps(k, at):
                dve.wait_ge(sem["side_ready"], w.at("side_ready", at + 1))
                own(nc.vector.tensor_scalar(rt, side[k][:], EPS, EPS, ALU.add, ALU.mult))
                nc.vector.tensor_tensor(rt, rt, side[k][:], ALU.add).then_inc(sem[f"side_read_{k}"], 1)

            def finish_mamba():
                for k in range(KD):
                    last = nc.vector.scalar_tensor_tensor(zm[:, k, :], zm[:, k, :], small[:, C_NORM + k:C_NORM + k + 1],
                                                          rs, ALU.mult, ALU.mult)
                last.then_inc(sem["normed_ready"], 1)
                w.add("normed_ready")

            def pair(s, j):
                gate, up_bank = 2 * (j % 2), 2 * (j % 2) + 1
                w.add("product_ready", 2)
                w.add(f"bank_read_{gate}")
                dve.wait_ge(sem["product_ready"], w.at("product_ready"))
                dve.wait_ge(sem[f"bank_read_{gate}"], w.at(f"bank_read_{gate}"))
                nc.vector.tensor_tensor(h[s % 2][:, j, :], main[up_bank][:], h[s % 2][:, j, :],
                                        ALU.mult).then_inc(sem[f"bank_read_{up_bank}"], 1)
                w.add(f"bank_read_{up_bank}")

            def magnitudes():
                w.add("magnitude_ready", 4)
                dve.wait_ge(sem["magnitude_ready"], w.at("magnitude_ready"))
                dve.wait_ge(sem["hidden_ready"], w.at("hidden_ready"))

            def compare_with(i):
                m, first = 3 - i, (0, 3, 5)[i]
                ins = nc.vector.tensor_tensor(cmp[:, first:first + m, :], ab[:, i:i + 1, :].broadcast_to([P, m, L]),
                                              ab[:, i + 1:4, :], ALU.is_ge)
                if i == 2:
                    ins.then_inc(sem["quad_compared"], 1)
                    w.add("quad_compared")
                    dve.wait_ge(sem["quad_compared"], w.at("quad_compared"))

            def count_wins():
                nc.vector.tensor_tensor(wins[:, 0:2, :], cmp[:, 1:4:2, :], cmp[:, 2:5:2, :], ALU.add)
                own(nc.vector.tensor_tensor(wins[:, 2:4, :], cmp[:, 1:3, :], cmp[:, 3:5, :], ALU.add))
                nc.vector.tensor_tensor(wins[:, 0, :], wins[:, 0, :], cmp[:, 0, :], ALU.add)
                nc.vector.tensor_tensor(wins[:, 1, :], wins[:, 1, :], cmp[:, 0, :], ALU.subtract)
                nc.vector.tensor_tensor(wins[:, 2, :], cmp[:, 5, :], wins[:, 2, :], ALU.subtract)
                own(nc.vector.tensor_tensor(wins[:, 3, :], cmp[:, 5, :], wins[:, 3, :], ALU.add))

            def select(s, members):
                tests = ((ALU.is_ge, 2.0), (ALU.is_ge, 1.0), (ALU.is_ge, 0.0), (ALU.is_le, 1.0))
                for i in members:
                    op, least = tests[i]
                    ins = nc.vector.scalar_tensor_tensor(h[s % 2][:, i, :], wins[:, i, :], least, h[s % 2][:, i, :], op, ALU.mult)
                    if i == 3:
                        ins.then_inc(sem["hidden_ready"], 1)
                        w.add("hidden_ready")

            def sparsify(s, q, part):
                if (q, part) == (1, 0):
                    magnitudes()
                    compare_with(0)
                if (q, part) == (1, 1):
                    compare_with(1)
                if (q, part) == (2, 0):
                    compare_with(2)
                if (q, part) == (2, 1):
                    count_wins()
                if (q, part) == (3, 0):
                    select(s - 1, (0, 1))
                if (q, part) == (3, 1):
                    select(s - 1, (2, 3))

            def add_down(body, s0, s, t):
                k = s0 + body.index(("down", s, t))
                src, dst = (G, G) if body.kinds[s] == "G" else (H if s % 4 == 0 else F, F)
                if s == 4 or (len(body.kinds) == 4 and s == 0):
                    dve.wait_ge(sem["res_f_free"], w.at("res_f_free"))
                if s % 4:
                    before = s0 + body.index(("down", s - 1, t))
                    dve.wait_ge(sem[f"side_read_{before % 2}"], w.at(f"side_read_{before % 2}", before // 2 + 1))
                dve.wait_ge(sem["side_ready"], w.at("side_ready", k + 1))
                nc.vector.scalar_tensor_tensor(dst[:, t, :], side[k % 2][:], 0.5, src[:, t, :],
                                               ALU.mult, ALU.add).then_inc(sem[f"side_read_{k % 2}"], 1)

            def convolve(body, s0, e, c0, v0):
                k = s0 + body.index(("in", e))
                dve.wait_ge(sem[f"side_read_{k % 2}"], w.at(f"side_read_{k % 2}", k // 2 + 1))
                dve.wait_ge(sem[f"u_stored_{e % 2}"], w.at(f"u_stored_{e % 2}", v0 + 16 * (e // 2)))
                c, x = cv[e % 2], up[e % 2]
                tap = lambda k: small[:, C_CW + e * DC + k:C_CW + e * DC + k + 1]
                own(nc.vector.tensor_scalar(c[:], x[:, 0:L], tap(0), small[:, C_CB + e:C_CB + e + 1], ALU.mult, ALU.add))
                for k in range(1, DC):
                    ins = nc.vector.scalar_tensor_tensor(c[:], x[:, k:k + L], tap(k), c[:], ALU.mult, ALU.add)
                    if k < DC - 1:
                        own(ins)
                ins.then_inc(sem["conv_ready"], 1)

            def scan(u0, u):
                dve.wait_ge(sem["decay_ready"], w.at("decay_ready", u0 + u + 1))
                dve.wait_ge(sem["input_ready"], w.at("input_ready", u0 + u + 1))
                dve.wait_ge(sem["weighted_ready"], w.at("weighted_ready", u0 + u - 1))
                nc.vector.tensor_tensor_scan(hs[u % 2][:], decay[u % RING][:], db[u % RING][:], 0.0, ALU.mult,
                                             ALU.add).then_inc(sem["state_ready"], 1)

            def times_c(u0, u):
                n, e = divmod(u, KE)
                if e == 0:
                    w.add(f"bc_loaded_{n % 2}", 32)
                    dve.wait_ge(sem[f"bc_loaded_{n % 2}"], w.at(f"bc_loaded_{n % 2}"))
                dve.wait_ge(sem["state_ready"], w.at("state_ready", u0 + u + 1))
                dve.wait_ge(sem["sum_ready"], w.at("sum_ready", u0 + u - RING + 1))
                nc.vector.tensor_tensor(pr[u % RING][:], hs[u % 2][:], Cb[n % 2][:], ALU.mult).then_inc(sem["weighted_ready"], 1)

            def first_terms(c):
                w.add(f"y_loaded_{c}", 16)
                dve.wait_ge(sem[f"y_loaded_{c}"], w.at(f"y_loaded_{c}"))
                for e in (2 * c, 2 * c + 1):
                    last = nc.vector.tensor_scalar(y[:, e, :], y[:, e, :], small[:, C_WD + e:C_WD + e + 1], None, ALU.mult)
                last.then_inc(sem["first_term_ready"], 1)

            def end_last(prev, u):
                s0 = w.count("side_ready") - len(prev.side)
                if prev.scan and u == ADD_OUT:
                    w.add("x1_loaded", 16)
                    dve.wait_ge(sem["x1_loaded"], w.at("x1_loaded"))
                    for t in range(KD):
                        w.add("product_ready")
                        dve.wait_ge(sem["product_ready"], w.at("product_ready"))
                        bank = BANK_OUT[t]
                        nc.vector.tensor_tensor(H[:, t, :], main[bank][:], H[:, t, :], ALU.add).then_inc(sem[f"bank_read_{bank}"], 1)
                        w.add(f"bank_read_{bank}")
                if prev.norm_next:
                    var_at = s0 + prev.index(("var", "G"))
                    if u == VARIANCE_G:
                        add_eps(var_at % 2, var_at)
                    if u == INVERSE_G:
                        inverse()
                    if u == SCALE_G:
                        scale()
                    if u == SPLIT_G:
                        split_input()
                if prev.kinds[-1] and u in ADD_LAST:
                    add_down(prev, s0, len(prev.kinds) - 1, ADD_LAST.index(u))
                if prev.kinds[-1] == "F" and u == LEAD - 1:
                    w.add("res_f_free", 16)

            def run_unit(u0, u):
                scan(u0, u)
                if u:
                    times_c(u0, u - 1)

            def run(body, prev):
                u0, s0, c0, v0 = (w.count(n) for n in ("state_ready", "side_ready", "conv_ready", "u_stored_0"))
                norms = {}
                for which in "FMG":
                    if ("mean", which) in body.side:
                        norms[which] = s0 + body.index(("mean", which)), s0 + body.index(("var", which))
                for u in range(body.lead):
                    end_last(prev, u)
                    if u < KE and u % 2 == 0:
                        first_terms(u // 2)
                    run_unit(u0, u)
                for tick in range(body.ticks + 1):
                    s, q = divmod(tick, STEP)
                    units = body.units_at[tick] if tick < body.ticks else range(0)
                    if "F" in norms and tick == FINISH_F:
                        dve.wait_ge(sem["product_ready"], w.at("product_ready", w.count("product_ready") + 2 * bool(body.kinds[s - 1])))
                        split_input()
                    for u in units[:1]:
                        run_unit(u0, u)
                    if tick:
                        for key in body.at_tick[tick - 1]:
                            if key[0] == "down":
                                add_down(body, s0, key[1], key[2])
                    if tick == body.ticks:
                        break
                    done = (s, q // 2 - 1) if q else (s - 1, 3)
                    if q % 2 == 0 and tick and body.kinds[done[0]]:
                        pair(*done)
                    if body.split and tick + AHEAD < body.units:
                        split_low(tick + AHEAD)
                    if "F" in norms:
                        mean_at, var_at = norms["F"]
                        if tick == NORM_F + 1:
                            centre(mean_at % 2, mean_at, H)
                        if tick == NORM_F + 3:
                            add_eps(var_at % 2, var_at)
                        if tick == NORM_F + 4:
                            inverse()
                        if tick == NORM_F + 6:
                            scale()
                    if "M" in norms:
                        mean_at, var_at = norms["M"]
                        if tick == NORM_M + 1:
                            centre(mean_at % 2, mean_at, G)
                        if tick == NORM_M + 3:
                            rms_eps(var_at % 2, var_at)
                        if tick == NORM_M + 4:
                            inverse()
                        if tick == NORM_M + 5:
                            finish_mamba()
                    if body.project:
                        e, odd = divmod(tick - PROJECT - 2, 2)
                        if not odd and 0 <= e < KE:
                            convolve(body, s0, e, c0, v0)
                    sparse = s and body.kinds[s - 1]
                    if sparse:
                        sparsify(s, q, 0)
                    for u in units[1:2]:
                        run_unit(u0, u)
                    if sparse:
                        sparsify(s, q, 1)
                    for u in units[2:]:
                        run_unit(u0, u)
                if body.scan:
                    times_c(u0, UNITS - 1)
                    for name in ("state_ready", "decay_ready", "input_ready", "weighted_ready", "sum_ready"):
                        w.add(name, UNITS)
                tail(body, s0, c0, v0, norms)
                if body.b == B:
                    for t in range(KD):
                        add_down(body, w.count("side_ready") - len(body.side), len(body.kinds) - 1, t)

            def tail(body, s0, c0, v0, norms):
                s = len(body.kinds) - 1
                if body.kinds[s]:
                    pair(s, 3)
                    for q in range(1, 4):
                        for part in range(2):
                            sparsify(s + 1, q, part)
                if body.scan:
                    dve.wait_ge(sem["sum_ready"], w.at("sum_ready"))
                    w.add("skip_loaded", 2 * 16)
                    dve.wait_ge(sem["skip_loaded"], w.at("skip_loaded"))
                    for e in range(KE):
                        nc.vector.tensor_tensor(y[:, e, :], y[:, e, :], skip_at[e], ALU.mult).then_inc(sem["gated_ready"], 1)
                    w.add("gated_ready", KE)
                if body.project:
                    for tick in range(body.ticks, PROJECT + 2 * KE + 2):
                        e, odd = divmod(tick - PROJECT - 2, 2)
                        if not odd and 0 <= e < KE:
                            convolve(body, s0, e, c0, v0)
                    w.add("conv_ready", KE)
                    for k in range(2):
                        w.add(f"u_stored_{k}", 16 * KE // 2)
                if body.project:
                    w.add("product_ready", 2)
                    for bank in (BANK_DT, BANK_BC):
                        w.add(f"bank_read_{bank}")
                if body.project:
                    bc_done = w.at("product_ready", w.count("product_ready") + KE // 2)
                    w.add("product_ready", KE)
                    for bank in BANK_DL:
                        w.add(f"bank_read_{bank}")
                    for half in range(2):
                        es = slice(half * KE // 2, (half + 1) * KE // 2)
                        w.add("log_ready")
                        dve.wait_ge(sem["log_ready"], w.at("log_ready"))
                        nc.vector.scalar_tensor_tensor(delta[:, es, :], delta[:, es, :], 0.0, soft[:],
                                                       ALU.max, ALU.add).then_inc(sem["delta_ready"], 1)
                        w.add("delta_ready")
                        dve.wait_ge(sem["delta_ready"], w.at("delta_ready"))
                        if half == 0:
                            dve.wait_ge(sem["product_ready"], bc_done)
                        nc.vector.tensor_tensor(du[:, es, :], delta[:, es, :], du[:, es, :], ALU.mult).then_inc(sem["du_ready"], 1)
                        if half == 0 and body.norm_next:
                            mean_at, _ = norms["G"]
                            centre(mean_at % 2, mean_at, G)
                w.add("side_ready", len(body.side))
                for k in range(2):
                    w.add(f"side_read_{k}", len(body.side) // 2)

            def head(x):
                at = w.count("side_ready")
                w.add("side_ready", 2)
                for k in range(2):
                    w.add(f"side_read_{k}")
                centre(at % 2, at, x)
                add_eps((at + 1) % 2, at + 1)
                inverse()
                scale()
                split_input()

            def prologue():
                w.add("res_f_free", 16)
                dve.wait_ge(sem["params_loaded"], 16 * PARAMS)
                dve.wait_ge(sem["const_ready"], 3)
                dve.wait_ge(sem["x_loaded"], 16)
                for n in range(AHEAD):
                    split_low(n)
                head(G)

            def epilogue(prev):
                for u in range(LEAD):
                    end_last(prev, u)
                head(H)

            batches(dve, w, run, prologue, epilogue)

        @block.gpsimd
        def _(pool):
            w = Walk()

            def scan_input(u0, u):
                n, e = divmod(u, KE)
                if u < KE and u % (KE // 2) == 0:
                    w.add("du_ready")
                    pool.wait_ge(sem["du_ready"], w.at("du_ready"))
                if e == 0:
                    w.add(f"bc_loaded_{n % 2}", 32)
                    pool.wait_ge(sem[f"bc_loaded_{n % 2}"], w.at(f"bc_loaded_{n % 2}"))
                pool.wait_ge(sem["state_ready"], w.at("state_ready", u0 + u - RING + 1))
                nc.gpsimd.tensor_tensor(db[u % RING][:], du[:, e, :], Bb[n % 2][:], ALU.mult).then_inc(sem["input_ready"], 1)

            def sum_states(u0, u):
                e = u % KE
                if u < KE and u % 2 == 0:
                    w.add("first_term_ready")
                    pool.wait_ge(sem["first_term_ready"], w.at("first_term_ready"))
                pool.wait_ge(sem["weighted_ready"], w.at("weighted_ready", u0 + u + 1))
                pool.wait_ge(sem["sum_ready"], w.at("sum_ready", u0 + u - KE + 1))
                nc.gpsimd.tensor_tensor(y[:, e, :], y[:, e, :], pr[u % RING][:], ALU.add).then_inc(sem["sum_ready"], 1)

            def run(body, prev):
                if not body.scan:
                    return
                u0 = w.count("state_ready")
                for u in range(UNITS):
                    scan_input(u0, u)
                    if u >= RING:
                        sum_states(u0, u - RING)
                for u in range(UNITS - RING, UNITS):
                    sum_states(u0, u)
                for name in ("state_ready", "weighted_ready", "sum_ready"):
                    w.add(name, UNITS)

            def prologue():
                nc.gpsimd.memset(F[:, 0, 0:1], 0.0).then_inc(sem["res_f_free"], 16)
                nc.gpsimd.memset(ones[:], 1.0 / D).then_inc(sem["const_ready"], 1)
                for k in range(2):
                    nc.gpsimd.memset(up[k][:, 0:DC - 1], 0.0).then_inc(sem["const_ready"], 1)

            batches(pool, w, run, prologue, lambda prev: None)


def _tiles(v):
    return v.reshape(-1, P).T


def kernel(L0_attn_x, L0_attn_norm_w, L0_attn_W_skip, L0_attn_W_in, L0_attn_conv_w, L0_attn_conv_b, L0_attn_Wd1,
           L0_attn_Wd2, L0_attn_bd2, L0_attn_WB, L0_attn_WC, L0_attn_A_log, L0_attn_W_D, L0_attn_W_out,
           L0_ffn_w_gate, L0_ffn_w_up, L0_ffn_w_down):
    import concourse.bacc as bacc
    from concourse.bass_utils import run_bass_kernel_spmd

    a = np.asarray
    x = a(L0_attn_x).transpose(0, 2, 1).reshape(B, KD, P, L).transpose(0, 2, 1, 3)
    cols = lambda v: a(v).reshape(KD, P, QUADS, P, 4).transpose(2, 4, 1, 0, 3)
    ffn = np.stack([cols(L0_ffn_w_gate), cols(L0_ffn_w_up)], axis=2)
    down = a(L0_ffn_w_down).reshape(QUADS, P, 4, KD, P).transpose(0, 3, 1, 2, 4)
    inner = lambda v: a(v).reshape(KE, P, KD, P).transpose(0, 3, 2, 1)
    mam = np.concatenate([inner(L0_attn_W_in), inner(L0_attn_W_skip)], axis=2)
    outer = a(L0_attn_W_out).reshape(KD, P, CHUNKS, 2, P).transpose(2, 4, 3, 0, 1).reshape(CHUNKS, P, 2 * KD, P)
    over_e = lambda v: a(v).T.reshape(KE, P, -1).transpose(1, 0, 2)
    wbc = over_e(np.concatenate([a(L0_attn_WB), a(L0_attn_WC)]))
    per_e = lambda v: a(v).reshape(KE, P, -1).transpose(1, 0, 2).reshape(P, -1)
    small = np.concatenate([_tiles(a(L0_attn_norm_w)), per_e(L0_attn_conv_w), _tiles(a(L0_attn_conv_b)),
                            _tiles(a(L0_attn_bd2)), per_e(L0_attn_A_log), _tiles(a(L0_attn_W_D))], axis=1)
    arrays = {"x_in": x, "ffn_w": ffn, "down_w": down, "mam_w": mam, "out_w": outer, "wdt_in": over_e(L0_attn_Wd1), "wbc_in": wbc,
              "wd2_in": a(L0_attn_Wd2).T, "small_in": small}
    arrays = {k: np.ascontiguousarray(v) for k, v in arrays.items()}

    nc = bacc.Bacc("TRN2", target_bir_lowering=False, num_devices=1)
    args = {k: nc.dram_tensor(k + "_dram", v.shape, mybir.dt.from_np(v.dtype), kind="ExternalInput").ap()
            for k, v in arrays.items()}
    out = nc.dram_tensor("out_dram", (B, P, KD, L), mybir.dt.float32, kind="ExternalOutput").ap()
    build(nc, out=out, **args)
    r = run_bass_kernel_spmd(nc, [{k + "_dram": v for k, v in arrays.items()}], core_ids=[0])
    got = r.results[0]["out_dram"]
    return np.ascontiguousarray(got.transpose(0, 2, 1, 3).reshape(B, D, L).transpose(0, 2, 1))
```
